# Optimizing a Trainium2 kernel written in Bass

```python
import numpy as np
import jax
import jax.numpy as jnp

def _softmax(x, axis=-1):
    return jax.nn.softmax(x, axis=axis)

def _gelu(x):
    return jax.nn.gelu(x, approximate=True)

def _silu(x):
    return jax.nn.silu(x)

def _sigmoid(x):
    return jax.nn.sigmoid(x)

def _layernorm(x, axis=-1, eps=1e-05):
    m = jnp.mean(x, axis=axis, keepdims=True)
    v = jnp.var(x, axis=axis, keepdims=True)
    return (x - m) / jnp.sqrt(v + eps)

def _scatter_add(tgt, idx, src, axis=0):
    return tgt.at[idx].add(src)

def _segment_sum(src, seg, n):
    return jax.ops.segment_sum(src, seg, n)
kernel_name = 'mk_xattn_ffn_d1_seqx_r8_d1fa62'

def setup_inputs(seed: int=0):
    np.random.seed(seed)
    _w = jnp.asarray

    def _rec_inputs():
        import jax
        import jax.numpy as jnp
        _rk = jax.random.key(seed)
        x = -0.0003929 + 0.9999 * jax.random.normal(jax.random.fold_in(_rk, 1), (32, 56, 128), jnp.float32)
        _lenS = 56 - jax.random.randint(jax.random.fold_in(_rk, 7), (32,), 0, max(1, 56 // 4) + 1, jnp.int32)
        _lenS2 = 1500 - jax.random.randint(jax.random.fold_in(_rk, 8), (32,), 0, max(1, 1500 // 4) + 1, jnp.int32)
        _ctx_1024P = jax.random.normal(jax.random.fold_in(_rk, 11), (32, 16, 128), jnp.float32)
        _ctx_1024c = jax.random.dirichlet(jax.random.fold_in(_rk, 511), 0.3 * jnp.ones((16,), jnp.float32), (32, 1500))
        _ctx_1024t = jnp.einsum('bsk,bkd->bsd', _ctx_1024c, _ctx_1024P)
        _ctx_1024t = _ctx_1024t * jax.lax.rsqrt(jnp.mean(jnp.square(_ctx_1024t)) + 1e-12) * 0.953939
        ctx_1024 = 2.81802e-05 + 1.00001 * (_ctx_1024t + 0.3 * jax.random.normal(jax.random.fold_in(_rk, 611), (32, 1500, 128), jnp.float32))
        _validS = jnp.arange(56)[None, :] < _lenS[:, None]
        _validS2 = jnp.arange(1500)[None, :] < _lenS2[:, None]
        _causal = jnp.tril(jnp.ones((56, 56), dtype=bool))
        mask_Bx1xS2_ik1 = jnp.where(jnp.broadcast_to(_validS2[:, None, :], (32, 1, 1500)), 1, 0).astype(jnp.int32)
        return (x, ctx_1024, mask_Bx1xS2_ik1)
    x, ctx_1024, mask_Bx1xS2_ik1 = _rec_inputs()

    def _L0_xattn_setup():
        import jax, jax.numpy as jnp
        import numpy as np
        B, NQ, NK = (8, 256, 256)
        DQ = DK = DV = 128
        EPS = 1e-05

        def _xavier(key, shape):
            fan_in, fan_out = (shape[0], shape[1])
            lim = float(np.sqrt(6.0 / (fan_in + fan_out)))
            return jax.random.uniform(key, shape, jnp.float32, -lim, lim)

        def _layernorm(x, g, b):
            mu = jnp.mean(x, axis=-1, keepdims=True)
            var = jnp.mean(jnp.square(x - mu), axis=-1, keepdims=True)
            return (x - mu) * jax.lax.rsqrt(var + EPS) * g + b
        key = jax.random.key(seed)
        ks = jax.random.split(key, 12)
        return {'Q': jax.random.normal(ks[0], (B, NQ, DQ), jnp.float32), 'K': jax.random.normal(ks[1], (B, NK, DK), jnp.float32), 'V': jax.random.normal(ks[2], (B, NK, DK), jnp.float32), 'pad_mask': jax.random.randint(ks[3], (B, 1, NK), 0, 2, jnp.int32), 'Wq': _xavier(ks[4], (DQ, DV)), 'bq': jnp.zeros((DV,), jnp.float32), 'Wk': _xavier(ks[5], (DK, DV)), 'bk': jnp.zeros((DV,), jnp.float32), 'Wv': _xavier(ks[6], (DK, DV)), 'bv': jnp.zeros((DV,), jnp.float32), 'Wo': _xavier(ks[7], (DV, DV)), 'bo': jnp.zeros((DV,), jnp.float32), 'g0': jnp.ones((DV,), jnp.float32), 'beta0': jnp.zeros((DV,), jnp.float32)}
    _L0_xattn_all = _L0_xattn_setup()
    _L0_xattn_in = {k: v for k, v in _L0_xattn_all.items() if k in ('Wq', 'bq', 'Wk', 'bk', 'Wv', 'bv', 'Wo', 'bo', 'g0', 'beta0')}
    del _L0_xattn_all

    def _L0_ffn_setup():
        import jax, jax.numpy as jnp
        import numpy as np
        D, H, O, E, TOPK = (128, 512, 128, 8, 2)
        B, S = (4, 128)
        key = jax.random.key(seed)
        ks = jax.random.split(key, 12)
        std = 0.02
        return {'hidden_states': jax.random.normal(ks[0], (B, S, D), dtype=jnp.float32), 'norm_weight': jnp.ones((D,), dtype=jnp.float32), 'router_w': jax.random.normal(ks[1], (E, D), dtype=jnp.float32) * std, 'sw1': jax.random.normal(ks[2], (D, H), dtype=jnp.float32) * (1.0 / np.sqrt(D)), 'sb1': jnp.zeros((H,), dtype=jnp.float32), 'sw2': jax.random.normal(ks[3], (H, O), dtype=jnp.float32) * (1.0 / np.sqrt(H)), 'sb2': jnp.zeros((O,), dtype=jnp.float32), 'ew1': jax.random.normal(ks[4], (E, D, H), dtype=jnp.float32) * (1.0 / np.sqrt(D)), 'eb1': jnp.zeros((E, H), dtype=jnp.float32), 'ew2': jax.random.normal(ks[5], (E, H, O), dtype=jnp.float32) * (1.0 / np.sqrt(H)), 'eb2': jnp.zeros((E, O), dtype=jnp.float32)}
    _L0_ffn_all = _L0_ffn_setup()
    _L0_ffn_in = {k: v for k, v in _L0_ffn_all.items() if k in ('norm_weight', 'router_w', 'sw1', 'sb1', 'sw2', 'sb2', 'ew1', 'eb1', 'ew2', 'eb2')}
    del _L0_ffn_all
    return {'x': x, 'ctx_1024': ctx_1024, 'mask_Bx1xS2_ik1': mask_Bx1xS2_ik1, 'L0_xattn_Wq': _L0_xattn_in['Wq'], 'L0_xattn_bq': _L0_xattn_in['bq'], 'L0_xattn_Wk': _L0_xattn_in['Wk'], 'L0_xattn_bk': _L0_xattn_in['bk'], 'L0_xattn_Wv': _L0_xattn_in['Wv'], 'L0_xattn_bv': _L0_xattn_in['bv'], 'L0_xattn_Wo': _L0_xattn_in['Wo'], 'L0_xattn_bo': _L0_xattn_in['bo'], 'L0_xattn_g0': _L0_xattn_in['g0'], 'L0_xattn_beta0': _L0_xattn_in['beta0'], 'L0_ffn_norm_weight': _L0_ffn_in['norm_weight'], 'L0_ffn_router_w': _L0_ffn_in['router_w'], 'L0_ffn_sw1': _L0_ffn_in['sw1'], 'L0_ffn_sb1': _L0_ffn_in['sb1'], 'L0_ffn_sw2': _L0_ffn_in['sw2'], 'L0_ffn_sb2': _L0_ffn_in['sb2'], 'L0_ffn_ew1': _L0_ffn_in['ew1'], 'L0_ffn_eb1': _L0_ffn_in['eb1'], 'L0_ffn_ew2': _L0_ffn_in['ew2'], 'L0_ffn_eb2': _L0_ffn_in['eb2']}

def reference(x, ctx_1024, mask_Bx1xS2_ik1, L0_xattn_Wq, L0_xattn_bq, L0_xattn_Wk, L0_xattn_bk, L0_xattn_Wv, L0_xattn_bv, L0_xattn_Wo, L0_xattn_bo, L0_xattn_g0, L0_xattn_beta0, L0_ffn_norm_weight, L0_ffn_router_w, L0_ffn_sw1, L0_ffn_sb1, L0_ffn_sw2, L0_ffn_sb2, L0_ffn_ew1, L0_ffn_eb1, L0_ffn_ew2, L0_ffn_eb2):
    import jax
    import jax.numpy as jnp

    def _L0_xattn_ref(Q, K, V, pad_mask, Wq, bq, Wk, bk, Wv, bv, Wo, bo, g0, beta0):
        import jax, jax.numpy as jnp
        import numpy as np
        B, NQ, NK = (8, 256, 256)
        DQ = DK = DV = 128
        EPS = 1e-05

        def _xavier(key, shape):
            fan_in, fan_out = (shape[0], shape[1])
            lim = float(np.sqrt(6.0 / (fan_in + fan_out)))
            return jax.random.uniform(key, shape, jnp.float32, -lim, lim)

        def _layernorm(x, g, b):
            mu = jnp.mean(x, axis=-1, keepdims=True)
            var = jnp.mean(jnp.square(x - mu), axis=-1, keepdims=True)
            return (x - mu) * jax.lax.rsqrt(var + EPS) * g + b
        q = Q @ Wq + bq
        k = K @ Wk + bk
        v = V @ Wv + bv
        scale = 1.0 / jnp.sqrt(jnp.float32(DV))
        scores = jnp.einsum('bqd,bkd->bqk', q, k) * scale
        scores = jnp.where(pad_mask == 0, jnp.float32(-1000000000.0), scores)
        w = jax.nn.softmax(scores, axis=-1)
        out = jnp.einsum('bqk,bkd->bqd', w, v)
        out = out @ Wo + bo
        out = _layernorm(out, g0, beta0)
        return out

    def _L0_ffn_ref(hidden_states, norm_weight, router_w, sw1, sb1, sw2, sb2, ew1, eb1, ew2, eb2):
        import jax, jax.numpy as jnp
        import numpy as np
        D, H, O, E, TOPK = (128, 512, 128, 8, 2)
        B, S = (4, 128)
        b, s, d = hidden_states.shape
        var = jnp.mean(jnp.square(hidden_states), axis=-1, keepdims=True)
        normed = hidden_states * jax.lax.rsqrt(var + 1e-08) * norm_weight
        shared = jnp.maximum(normed @ sw1 + sb1, 0.0) @ sw2 + sb2
        flat = normed.reshape(-1, d)
        T = flat.shape[0]
        probs = jax.nn.sigmoid(flat @ router_w.T)
        scores, idx = jax.lax.top_k(probs, TOPK)
        w = scores / (jnp.sum(scores, axis=-1, keepdims=True) + 1e-06)
        comb = jnp.zeros((T, E), dtype=flat.dtype)
        comb = comb.at[jnp.arange(T)[:, None], idx].add(w)
        h = jnp.maximum(jnp.einsum('td,edh->teh', flat, ew1) + eb1[None, :, :], 0.0)
        eo = jnp.einsum('teh,eho->teo', h, ew2) + eb2[None, :, :]
        routed = jnp.einsum('teo,te->to', eo, comb)
        return shared + routed.reshape(b, s, -1)
    x = x + _L0_xattn_ref(_layernorm(x, axis=-1), ctx_1024, ctx_1024, mask_Bx1xS2_ik1, L0_xattn_Wq, L0_xattn_bq, L0_xattn_Wk, L0_xattn_bk, L0_xattn_Wv, L0_xattn_bv, L0_xattn_Wo, L0_xattn_bo, L0_xattn_g0, L0_xattn_beta0)
    x = x + _L0_ffn_ref(_layernorm(x, axis=-1), L0_ffn_norm_weight, L0_ffn_router_w, L0_ffn_sw1, L0_ffn_sb1, L0_ffn_sw2, L0_ffn_sb2, L0_ffn_ew1, L0_ffn_eb1, L0_ffn_ew2, L0_ffn_eb2)
    return x

_drawn_inputs = setup_inputs


def setup_inputs(seed=0):
    import zlib

    import numpy as np

    out = dict(_drawn_inputs(seed))
    spreads = {'L0_xattn_bq': (0.0, 0.1),
     'L0_xattn_bk': (0.0, 0.8),
     'L0_xattn_bv': (0.0, 0.1),
     'L0_xattn_bo': (0.0, 0.1),
     'L0_xattn_g0': (1.0, 0.2),
     'L0_xattn_beta0': (0.0, 0.1),
     'L0_ffn_norm_weight': (1.0, 0.2),
     'L0_ffn_sb1': (0.0, 0.1),
     'L0_ffn_sb2': (0.0, 0.1),
     'L0_ffn_eb1': (0.0, 0.276),
     'L0_ffn_eb2': (0.0, 0.1)}
    factors = {}
    for name, (base, spread) in spreads.items():
        noise = np.random.default_rng([zlib.crc32(name.encode()), seed]).standard_normal(out[name].shape)
        drawn = base * np.exp(spread * noise) if base else spread * noise
        out[name] = jnp.asarray(drawn.astype(out[name].dtype))
    for name, factor in factors.items():
        out[name] = (out[name] * factor).astype(out[name].dtype)
    return out
```

```python
import concourse.bass as bass
from concourse import mybir
from contextlib import ExitStack

F32 = mybir.dt.float32
F32R = mybir.dt.float32r
BF16 = mybir.dt.bfloat16
I32 = mybir.dt.int32
ALU = mybir.AluOpType
ACT = mybir.ActivationFunctionType
AX = mybir.AxisListType

P = 128
B, SQ, D = 32, 56, 128
SK = 1500
HID = 512
NE = 8
NX = NE + 1
HALF = 64
PAIRS = B // 2
GP = 4
GROUPS = PAIRS // GP
GT = GP * 2 * SQ
PT2 = 2 * SQ
KC = (SK + P - 1) // P
KF = KC - 1
KT = SK - KF * P
SC = 3
SN = SK // SC
MC = HID // P
UNITS = NX * MC
LAG = 3
STEPS = UNITS + LAG
HR = 4
SCALE = 1.0 / float(D) ** 0.5
MASKED = -1.0e30
LN_EPS = 1e-5
RMS_EPS = 1e-8
PLAN = [(0, 4), (5, 6), (5, 6), (6, 7)]
assert sum(a + b for a, b in PLAN) == STEPS


def build(nc, x, ctx_in, ctxT_in, mask, WqT, bq, WkT, bk, WvT, bv, Wo, bo, g0, beta0, nw, rw,
          sw1, sw2, sb2, b1_in, ew1, ew2, eb2, ident_in, out):
    es = ExitStack()
    with es:
        def sb(name, shape, dt=F32):
            return es.enter_context(nc.sbuf_tensor(name, shape, dt))

        def ps(name, shape, dt=F32):
            return es.enter_context(nc.psum_tensor(name, shape, dt))

        def sem(name):
            return es.enter_context(nc.semaphore(name))

        mbias_d = nc.dram_tensor("mbias_scratch", [B, SK], BF16, kind="Internal").ap()
        comb_d = nc.dram_tensor("comb_scratch", [GROUPS, NE * GT], F32, kind="Internal").ap()

        ident = sb("ident_sb", [P, P])
        X = sb("X_sb", [P, PAIRS, D])
        ctxT = sb("ctxT_sb", [P, 2, 2, SK])
        ctxN = sb("ctxN_sb", [P, 2, 2, KC, D])
        mb = sb("mb_sb", [P, 2, SK], BF16)
        S = sb("S_sb", [P, SK])
        PT = sb("PT_sb", [P, KC, P])
        w1h = sb("w1h_sb", [P, NX, HID], F32R)
        w1l = sb("w1l_sb", [P, NX, HID], F32R)
        w2h = sb("w2h_sb", [P, NX, MC, D], F32R)
        w2l = sb("w2l_sb", [P, NX, MC, D], F32R)
        comb_bc = sb("comb_bc_sb", [P, NE * GT])
        qT = sb("qT_sb", [P, GP * P])
        xn0 = sb("xn0_sb", [P, GP, D])
        xn0T = sb("xn0T_sb", [P, GP * P])
        xn = sb("xn_sb", [P, GP, D])
        xT = sb("xT_sb", [P, GT])
        xh = sb("xh_sb", [P, GT], F32R)
        xl = sb("xl_sb", [P, GT], F32R)
        Hf = sb("Hf_sb", [P, 2, GT])
        Hh = sb("Hh_sb", [P, HR, GT], F32R)
        Hl = sb("Hl_sb", [P, HR, GT], F32R)
        acc = sb("acc_sb", [P, GP, 2, HALF])
        tmp = sb("tmp_sb", [P, 2, GT])
        o1 = sb("o1_sb", [P, D])
        o1T = sb("o1T_sb", [P, P])
        a1f = sb("a1f_sb", [P, 4 * D], BF16)
        a1 = a1f[:, 0:2 * D].bitcast(F32)
        a2 = a1f[:, 2 * D:4 * D].bitcast(F32)
        a3 = sb("a3_sb", [P, D])
        Wqk = sb("Wqk_sb", [P, D])
        Wvo = sb("Wvo_sb", [P, D])
        WqT_s, WkT_s, WvT_s = (tmp[:, 0, i * D:(i + 1) * D] for i in range(3))
        Wo_s, bo_bc, bv_rep = (tmp[:, 1, i * D:(i + 1) * D] for i in range(3))
        bq_rep, zero_pp = (Hf[:, 0, i * D:(i + 1) * D] for i in range(2))
        bvo_bc = sb("bvo_bc_sb", [P, D])
        g0_bc = sb("g0_bc_sb", [P, D])
        beta_bc = sb("beta_bc_sb", [P, D])
        cols = sb("cols_sb", [P, 8])
        rwT = sb("rwT_sb", [P, NE])
        b1 = sb("b1_sb", [P, UNITS])
        b2 = sb("b2_sb", [NE + 1, D])
        combT = sb("combT_sb", [NE + 1, GT])
        mi = S[:, 0:B * SK // P].bitcast(I32)
        mf = a1f[:, 0:B * SK // P]
        mneg = sb("mneg_sb", [P, GP])
        low = sb("low_sb", [PT2, NE, NE])
        st0 = sb("st0_sb", [P, GP, 6])
        mv0 = sb("mv0_sb", [P, GP, 2])
        ve0 = sb("ve0_sb", [P, GP])
        rs0 = sb("rs0_sb", [P, GP])
        cq = sb("cq_sb", [P, GP])
        pmax = sb("pmax_sb", [P, SC])
        mfull = sb("mfull_sb", [P, 1])
        mc = sb("mc_sb", [P, 1])
        scrap = sb("scrap_sb", [1, 32])
        nbias = sb("nbias_sb", [P, 1])
        rsum = sb("rsum_sb", [P, SC])
        rtot = sb("rtot_sb", [P, 1])
        rinv = sb("rinv_sb", [P, 1])
        st1 = sb("st1_sb", [P, 6])
        mv1 = sb("mv1_sb", [P, 2])
        ve1 = sb("ve1_sb", [P, 1])
        rs1 = sb("rs1_sb", [P, 1])
        st2 = sb("st2_sb", [P, 6])
        mv2 = sb("mv2_sb", [P, 2])
        ve2 = sb("ve2_sb", [P, 1])
        rs2 = sb("rs2_sb", [P, 1])
        el = sb("el_sb", [PT2, GP, NE])
        el1 = sb("el1_sb", [PT2, GP, NE])
        pr = sb("pr_sb", [PT2, GP, NE])
        cmpg = sb("cmpg_sb", [PT2, GP, NE, NE])
        cmpe = sb("cmpe_sb", [PT2, GP, NE, NE])
        rank = sb("rank_sb", [PT2, GP, NE])
        selp = sb("selp_sb", [PT2, GP, NE])
        ssum = sb("ssum_sb", [PT2, GP])
        sden = sb("sden_sb", [PT2, GP])
        sinv = sb("sinv_sb", [PT2, GP])
        comb = sb("comb_sb", [PT2, GP, NE])

        SB_ = [ps(f"S{c}_ps", [P, 512]) for c in range(SC)]
        UB = [ps(f"U{c}_ps", [P, 512]) for c in range(2)]
        YB = ps("Y_ps", [P, 512])
        OB = ps("O_ps", [P, 512])
        MB = ps("M_ps", [P, 512])

        small_in = sem("small_in")
        b2_here = sem("b2_here")
        x_cleared = sem("x_cleared")
        mask_in = sem("mask_in")
        mbias_made = sem("mbias_made")
        mbias_out = sem("mbias_out")
        ctxT_here = [sem(f"ctxT_here{i}") for i in range(2)]
        ctxN_here = [sem(f"ctxN_here{i}") for i in range(2)]
        mb_here = [sem(f"mb_here{i}") for i in range(2)]
        w_here = [sem(f"w_here{i}") for i in range(2)]
        w_split = sem("w_split")
        pool_init = sem("pool_init")
        dve_init = sem("dve_init")
        setup_mm = sem("setup_mm")
        setup_ev = sem("setup_ev")
        scored = sem("scored")
        masked = sem("masked")
        shifted = sem("shifted")
        exped = sem("exped")
        p_turned = sem("p_turned")
        p_copied = sem("p_copied")
        pv_done = sem("pv_done")
        o1_made = sem("o1_made")
        o1_turned = sem("o1_turned")
        o1T_made = sem("o1T_made")
        projected = sem("projected")
        a1_made = sem("a1_made")
        xn_turned = sem("xn_turned")
        routed = sem("routed")
        comb_turned = sem("comb_turned")
        xn0_turned = sem("xn0_turned")
        xn0T_made = sem("xn0T_made")
        q_projected = sem("q_projected")
        q_made = sem("q_made")
        c_projected = sem("c_projected")
        y_turned = sem("y_turned")
        x0_stat = sem("x0_stat")
        x0_rstd = sem("x0_rstd")
        x0_norm = sem("x0_norm")
        xb_made = sem("xb_made")
        cq_made = sem("cq_made")
        a_stat = sem("a_stat")
        a_rstd = sem("a_rstd")
        a_norm = sem("a_norm")
        a3_made = sem("a3_made")
        x1_made = sem("x1_made")
        x1_stat = sem("x1_stat")
        x1_rstd = sem("x1_rstd")
        xn_made = sem("xn_made")
        xT_made = sem("xT_made")
        x_split = sem("x_split")
        el_made = sem("el_made")
        comb_made = sem("comb_made")
        combT_made = sem("combT_made")
        comb_out = sem("comb_out")
        comb_here = sem("comb_here")
        upped = sem("upped")
        relued = sem("relued")
        h_hi = sem("h_hi")
        h_split = sem("h_split")
        downed = sem("downed")
        y_read = sem("y_read")
        acc_added = sem("acc_added")
        out_made = sem("out_made")
        out_sent = sem("out_sent")
        dve_step = sem("dve_step")

        def run_bodies(eng, body):
            body("first", 0)
            with eng.Fori(1, GROUPS - 1) as g:
                body("mid", g)
            body("late", GROUPS - 1)
            body("last", GROUPS)

        def has(kind, what):
            if what == "attn":
                return kind != "last"
            if what == "ffn":
                return kind != "first"
            if what == "next_q":
                return kind in ("first", "mid")

        def has_tail(kind, q):
            return not (kind == "first" and q == 0) and not (kind == "last" and q)

        def steps_of(q):
            n0 = sum(a + b for a, b in PLAN[:q])
            a, b = PLAN[q]
            return list(range(n0, n0 + a)), list(range(n0 + a, n0 + a + b))

        block = es.enter_context(nc.Block())

        SMALL = 18 * 16

        @block.sync
        def _(sp):
            def small(dst, src):
                sp.dma_start(dst, src).then_inc(small_in, 16)

            def spread(v, n=P):
                return v.rearrange("(o d) -> o d", o=1).broadcast_to([n, D])

            def load_pair(p, slot):
                sp.dma_start(ctxT[:, slot, :, :], ctxT_in[bass.ds(p * 2, 2), :, :].rearrange("b d k -> d b k"))\
                    .then_inc(ctxT_here[slot], 16)
                for b in range(2):
                    sp.dma_start(mb[b * HALF:(b + 1) * HALF, slot, :],
                                 mbias_d[bass.ds(p * 2 + b, 1), :].broadcast_to([HALF, SK]))\
                        .then_inc(mb_here[slot], 16)
                src = ctx_in[bass.ds(p * 2, 2), :, :]
                sp.dma_start(ctxN[:, slot, :, 0:KF, :],
                             src[:, 0:KF * P, :].rearrange("b (k c) d -> k b c d", c=KF)).then_inc(ctxN_here[slot], 16)
                sp.dma_start(ctxN[0:KT, slot, :, KF, :],
                             src[:, KF * P:SK, :].rearrange("b k d -> k b d")).then_inc(ctxN_here[slot], 16)

            sp.dma_start(mi, mask.rearrange("b o k -> (b o k)").rearrange("(p n) -> p n", p=P)).then_inc(mask_in, 16)
            xv = x.rearrange("(p b) i d -> b i p d", b=2)
            for n, (lo, hi) in enumerate(((0, GP), (GP, PAIRS))):
                sp.wait_ge(x_cleared, n + 1)
                for b in range(2):
                    small(X[b * HALF:b * HALF + SQ, lo:hi, :], xv[b][:, lo:hi, :])
                if n == 0:
                    small(ident[:, :], ident_in)
                    small(WqT_s, WqT)
                    small(WkT_s, WkT)
                    for i, v in enumerate((bq, bk, bv, nw)):
                        small(cols[:, i:i + 1], v.rearrange("(d o) -> d o", o=1))
                    small(WvT_s, WvT)
                    small(Wo_s, Wo)
                    sp.wait_ge(mbias_made, 1)
                    sp.dma_start(mbias_d.rearrange("b k -> (b k)").rearrange("(p n) -> p n", p=P), mf)\
                        .then_inc(mbias_out, 16)
            small(bo_bc, spread(bo))
            small(g0_bc[:, :], spread(g0))
            small(beta_bc[:, :], spread(beta0))
            small(rwT[:, :], rw)
            small(b1[:, :], b1_in)
            sp.wait_ge(mbias_out, 16)
            load_pair(0, 0)
            load_pair(1, 1)
            sp.dma_start(b2[0:NE, :], eb2).then_inc(b2_here, 16)
            sp.dma_start(b2[NE:NE + 1, :], sb2.rearrange("(o d) -> o d", o=1)).then_inc(b2_here, 16)

            ov = out.rearrange("(p b) i d -> b i p d", b=2)

            def body(kind, g):
                for q in range(GP):
                    if q == 1 and has(kind, "ffn"):
                        f = g - 1
                        sp.wait_ge(combT_made, g)
                        if kind == "mid":
                            sp.wait_ge(w_split, 4 * NX)
                        sp.dma_start(comb_d[bass.ds(f, 1), :].rearrange("o (e t) -> (o e) t", e=NE),
                                     combT[0:NE, :]).then_inc(comb_out, 16)
                        sp.wait_ge(comb_out, g * 16)
                        sp.dma_start(comb_bc[:, :], comb_d[bass.ds(f, 1), :].broadcast_to([P, NE * GT]))\
                            .then_inc(comb_here, 16)
                    if has(kind, "attn") and not (kind == "late" and q >= 2):
                        p = g * GP + q
                        sp.wait_ge(scored, (p + 1) * SC)
                        sp.wait_ge(masked, (p + 1) * SC)
                        sp.wait_ge(pv_done, p + 1)
                        load_pair(p + 2, q % 2)
                if has(kind, "ffn"):
                    f = g - 1
                    sp.wait_ge(out_made, g + 1)
                    for b in range(2):
                        sp.dma_start(ov[b][:, bass.ds(f * GP, GP), :],
                                     X[b * HALF:b * HALF + SQ, bass.ds(f * GP, GP), :]).then_inc(out_sent, 16)

            run_bodies(sp, body)
            sp.wait_ge(out_sent, GROUPS * 32)

        def pair_of(t, p):
            return t[:, bass.ds(p, 1), :].rearrange("p o d -> p (o d)")

        @block.gpsimd
        def _(pool):
            pool.memset(X[:, 0:GP, :], 0.0).then_inc(x_cleared, 1)
            pool.memset(X[:, GP:PAIRS, :], 0.0).then_inc(x_cleared, 1)
            pool.memset(mneg[:, :], -0.5).then_inc(pool_init, 1)
            pool.memset(low[:, :, :], 1.0).then_inc(pool_init, 1)
            pool.wait_ge(pool_init, 2)
            pool.affine_select(out=low[:, :, :], in_=low[:, :, :], compare_op=ALU.is_ge, fill=0.0, base=-1,
                               pattern=[[1, NE], [-1, NE]], channel_multiplier=0).then_inc(pool_init, 1)

            def next_x(g, at):
                pool.wait_ge(x0_stat, at)
                pool.tensor_tensor(rs0[:, :], ve0[:, :], mneg[:, :], ALU.pow).then_inc(x0_rstd, 1)
                pool.wait_ge(x0_norm, at)
                for j in range(GP):
                    xj = pair_of(X, g * GP + j)
                    pool.tensor_tensor(xj, xj, beta_bc[:, :], ALU.add).then_inc(xb_made, 1)

            def split_weights(e):
                stage = comb_bc[:, (e % 2) * 2 * HID:(e % 2 + 1) * 2 * HID]
                flat = "p m d -> p (m d)"
                pool.wait_ge(w_here[e % 2], 32 * (e // 2 + 1))
                pool.tensor_copy(w1h[:, e, :], stage[:, 0:HID]).then_inc(w_split, 1)
                pool.tensor_copy(w2h[:, e, :, :].rearrange(flat), stage[:, HID:2 * HID]).then_inc(w_split, 1)
                pool.wait_ge(w_split, 4 * e + 2)
                pool.tensor_tensor(w1l[:, e, :], stage[:, 0:HID], w1h[:, e, :].bitcast(F32), ALU.subtract)\
                    .then_inc(w_split, 1)
                pool.tensor_tensor(w2l[:, e, :, :].rearrange(flat), stage[:, HID:2 * HID],
                                   w2h[:, e, :, :].rearrange(flat).bitcast(F32), ALU.subtract).then_inc(w_split, 1)

            def load_weights(e):
                s1, s2 = (sw1, sw2) if e == 0 else (ew1[e - 1], ew2[e - 1])
                if e >= 2:
                    pool.wait_ge(w_split, 4 * (e - 1))
                base = (e % 2) * 2 * HID
                pool.dma_start(comb_bc[:, base:base + HID], s1).then_inc(w_here[e % 2], 16)
                pool.dma_start(comb_bc[:, base + HID:base + 2 * HID].rearrange("p (m d) -> p m d", m=MC),
                               s2.rearrange("(m p) d -> p m d", m=MC)).then_inc(w_here[e % 2], 16)

            load_weights(0)
            load_weights(1)
            pool.wait_ge(small_in, SMALL)
            next_x(0, 1)

            def tail(g, q):
                p1 = g * GP + q
                pool.wait_ge(a_stat, p1)
                pool.tensor_tensor(rs1[:, :], ve1[:, :], mneg[:, 0:1], ALU.pow).then_inc(a_rstd, 1)
                pool.wait_ge(a_norm, p1)
                pool.tensor_tensor(a3[:, :], a2, g0_bc[:, :], ALU.mult).then_inc(a3_made, 1)
                pool.wait_ge(a3_made, p1)
                pool.wait_ge(xb_made, p1)
                pool.tensor_tensor(pair_of(X, p1 - 1), pair_of(X, p1 - 1), a3[:, :], ALU.add).then_inc(x1_made, 1)
                pool.wait_ge(x1_stat, p1)
                pool.tensor_tensor(rs2[:, :], ve2[:, :], mneg[:, 0:1], ALU.pow).then_inc(x1_rstd, 1)

            def add_expert(g, e):
                f = g - 1
                pool.wait_ge(y_read, f * NX + e + 1)
                if e > 1:
                    pool.wait_ge(acc_added, f * NE + e - 1)
                a = acc[:, :, :, 0:SQ].rearrange("p j b i -> p (j b) i")
                pool.tensor_tensor(a, a, tmp[:, e % 2, :].rearrange("p (c i) -> p c i", i=SQ), ALU.add)\
                    .then_inc(acc_added, 1)

            def body(kind, g):
                for q in range(GP):
                    if kind == "first":
                        for e in range((NX * q) // GP, (NX * (q + 1)) // GP):
                            split_weights(e)
                            if e + 2 < NX:
                                load_weights(e + 2)
                    if has_tail(kind, q):
                        tail(g, q)
                    if q == 2 and has(kind, "next_q"):
                        next_x(g + 1, g + 2)
                    if has(kind, "ffn"):
                        sa, sb_ = steps_of(q)
                        for n in sa + sb_:
                            e, m = (n - LAG) // MC, (n - LAG) % MC
                            if m == MC - 1 and e >= 1:
                                add_expert(g, e)

            run_bodies(pool, body)

        @block.tensor
        def _(pe):
            mm, tr = pe.matmul, pe.transpose

            pe.wait_ge(small_in, SMALL)
            pe.wait_ge(dve_init, 3)
            mm(SB_[0][:, 0:D], WqT_s, WkT_s, start=True, stop=True).then_inc(setup_mm, 1)
            mm(SB_[1][:, 0:D], WvT_s, Wo_s, start=True, stop=True).then_inc(setup_mm, 1)
            mm(SB_[2][:, 0:D], bv_rep, Wo_s, start=True, stop=True).then_inc(setup_mm, 1)
            mm(UB[0][:, 0:1], WkT_s, cols[:, 0:1], start=True, stop=True)
            mm(UB[0][:, 1:2], WqT_s, cols[:, 1:2], start=True, stop=True)
            mm(UB[0][:, 2:3], bq_rep, cols[:, 1:2], start=True, stop=True).then_inc(setup_mm, 1)

            def next_q(g1):
                pe.wait_ge(x0_norm, g1)
                for j in range(GP):
                    last = tr(MB[:, j * P:(j + 1) * P], xn0[:, j, :], ident[:, :])
                last.then_inc(xn0_turned, 1)

            def next_q2(g1):
                pe.wait_ge(xn0T_made, g1)
                mm(MB[:, :], Wqk[:, :], xn0T[:, :], start=True, stop=True).then_inc(q_projected, 1)
                pe.wait_ge(q_made, g1)
                for j in range(GP):
                    last = mm(MB[:, j:j + 1], xn0T[:, j * P:(j + 1) * P], cols[:, 5:6], start=True, stop=True)
                last.then_inc(c_projected, 1)

            next_q(1)
            pe.wait_ge(setup_ev, 4)
            next_q2(1)

            def scores(kind, g, q):
                p, slot = g * GP + q, q % 2
                if q == 0:
                    pe.wait_ge(q_made, g + 1)
                pe.wait_ge(ctxT_here[slot], 16 * (g * (GP // 2) + q // 2 + 1))
                for c in range(SC):
                    if not (kind == "first" and q == 0):
                        pe.wait_ge(p_copied, (p - 1) * SC + c + 1)
                    for b in range(2):
                        last = mm(SB_[c][b * HALF:(b + 1) * HALF, 0:SN],
                                  qT[:, q * P + b * HALF:q * P + (b + 1) * HALF],
                                  ctxT[:, slot, b, c * SN:(c + 1) * SN], start=True, stop=True)
                    last.then_inc(scored, 1)

            def turn_p(g, q):
                p = g * GP + q
                pe.wait_ge(exped, (p + 1) * SC)
                for c in range(SC):
                    for i in range(4):
                        k = c * 4 + i
                        if k < KF:
                            last = tr(SB_[c][:, i * P:(i + 1) * P], S[:, k:KF * P:KF], ident[:, :])
                        else:
                            last = tr(SB_[c][0:KT, i * P:(i + 1) * P], S[:, KF * P:SK], ident[:, :])
                    last.then_inc(p_turned, 1)

            def pv(kind, g, q):
                p, slot = g * GP + q, q % 2
                pe.wait_ge(ctxN_here[slot], 32 * (g * (GP // 2) + q // 2 + 1))
                if not (kind == "first" and q == 0):
                    pe.wait_ge(o1_made, p)
                for k in range(KC):
                    if k % 4 == 0:
                        pe.wait_ge(p_copied, p * SC + k // 4 + 1)
                    n = P if k < KF else KT
                    for b in range(2):
                        last = mm(OB[b * HALF:(b + 1) * HALF, 0:D], PT[0:n, k, b * HALF:(b + 1) * HALF],
                                  ctxN[0:n, slot, b, k, :], start=(k == 0), stop=(k == KC - 1))
                last.then_inc(pv_done, 1)

            def turn_o(kind, g, q):
                p1 = g * GP + q
                pe.wait_ge(o1_made, p1)
                if q == 0:
                    pe.wait_ge(out_made, g)
                    if kind != "last":
                        pe.wait_ge(cq_made, g + 1)
                elif q == 1 and kind == "first":
                    pe.wait_ge(cq_made, 1)
                elif q == 1:
                    pe.wait_ge(combT_made, g)
                else:
                    pe.wait_ge(a1_made, p1 - 1)
                tr(MB[:, 0:P], o1[:, :], ident[:, :]).then_inc(o1_turned, 1)

            def proj(g, q):
                p1 = g * GP + q
                pe.wait_ge(o1T_made, p1)
                mm(MB[:, 0:D], o1T[:, :], Wvo[:, :], start=True, stop=True).then_inc(projected, 1)

            def turn_x(g):
                pe.wait_ge(xn_made, g * GP)
                pe.wait_ge(a1_made, g * GP)
                for j in range(GP):
                    last = tr(MB[:, j * P:(j + 1) * P], xn[:, j, :], ident[:, :])
                last.then_inc(xn_turned, 1)

            def route(g):
                pe.wait_ge(xT_made, g)
                for j in range(GP):
                    last = mm(MB[0:PT2, j * NE:(j + 1) * NE], xT[:, j * PT2:(j + 1) * PT2], rwT[:, :],
                              start=True, stop=True)
                last.then_inc(routed, 1)

            def turn_comb(g):
                pe.wait_ge(comb_made, g)
                for j in range(GP):
                    last = tr(MB[0:NE, j * PT2:(j + 1) * PT2], comb[:, j, :], ident[0:PT2, 0:PT2])
                last.then_inc(comb_turned, 1)

            def step(g, n):
                f = g - 1
                if n < UNITS:
                    e, m = n // MC, n % MC
                    if n == 0:
                        pe.wait_ge(x_split, 2 * g)
                        pe.wait_ge(w_split, 4 * NX)
                    if n >= 2:
                        pe.wait_ge(relued, f * UNITS + n - 1)
                    u = UB[n % 2][:, 0:GT]
                    wh, wl = w1h[:, e, m * P:(m + 1) * P], w1l[:, e, m * P:(m + 1) * P]
                    mm(u, wh, xh[:, :], start=True, stop=False)
                    mm(u, wh, xl[:, :], start=False, stop=False)
                    mm(u, wl, xh[:, :], start=False, stop=True).then_inc(upped, 1)
                u = n - LAG
                if u >= 0:
                    e, m, r = u // MC, u % MC, u % HR
                    if m == 0 and e > 0:
                        pe.wait_ge(y_read, f * NX + e)
                    pe.wait_ge(h_split, f * UNITS + u + 1)
                    y = YB[:, 0:GT]
                    mm(y, w2h[:, e, m, :], Hh[:, r, :], start=(m == 0), stop=False)
                    mm(y, w2h[:, e, m, :], Hl[:, r, :], start=False, stop=False)
                    i = mm(y, w2l[:, e, m, :], Hh[:, r, :], start=False, stop=(m == MC - 1 and e > 0))
                    if m == MC - 1 and e == 0:
                        pe.wait_ge(combT_made, g)
                        pe.wait_ge(b2_here, 32)
                        i = mm(y, b2[:, :], combT[:, :], start=False, stop=True)
                    i.then_inc(downed, 1)

            def turn_y(g):
                pe.wait_ge(acc_added, g * NE)
                for j in range(GP):
                    last = tr(MB[:, j * P:(j + 1) * P], acc[:, j, :, :].rearrange("p b i -> p (b i)"), ident[:, :])
                last.then_inc(y_turned, 1)

            def body(kind, g):
                for q in range(GP):
                    sa, sb_ = steps_of(q)
                    attn, ffn, t = has(kind, "attn"), has(kind, "ffn"), has_tail(kind, q)
                    if attn:
                        scores(kind, g, q)
                    if q == 1 and ffn:
                        turn_comb(g)
                    if t:
                        turn_o(kind, g, q)
                    if q == 0:
                        if attn:
                            turn_p(g, q)
                        if t:
                            proj(g, q)
                        if attn:
                            pv(kind, g, q)
                        if ffn:
                            turn_x(g)
                            route(g)
                            for n in sb_:
                                step(g, n)
                    else:
                        if ffn:
                            for n in sa:
                                step(g, n)
                        if t:
                            proj(g, q)
                        if attn:
                            turn_p(g, q)
                        if ffn:
                            for n in sb_:
                                step(g, n)
                        if attn:
                            pv(kind, g, q)
                    if q == GP - 1 and has(kind, "next_q"):
                        pe.wait_ge(a1_made, g * GP + q)
                        next_q(g + 2)
                        next_q2(g + 2)
                if ffn:
                    if has(kind, "next_q"):
                        pe.wait_ge(cq_made, g + 2)
                    turn_y(g)

            run_bodies(pe, body)

        @block.scalar
        def _(act):
            A = nc.scalar.activation

            def copy(dst, src):
                return A(dst, src, ACT.Copy)

            act.wait_ge(setup_mm, 1)
            copy(Wqk[:, :], SB_[0][:, 0:D]).then_inc(setup_ev, 1)
            act.wait_ge(setup_mm, 2)
            copy(Wvo[:, :], SB_[1][:, 0:D]).then_inc(setup_ev, 1)
            act.wait_ge(setup_mm, 3)
            copy(bvo_bc[:, :], SB_[2][:, 0:D]).then_inc(setup_ev, 1)
            act.wait_ge(setup_mm, 4)
            copy(cols[:, 4:7], UB[0][:, 0:3]).then_inc(setup_ev, 1)

            def take_q(g1):
                act.wait_ge(xn0_turned, g1)
                copy(xn0T[:, :], MB[:, :]).then_inc(xn0T_made, 1)
                act.wait_ge(q_projected, g1)
                A(qT[:, :], MB[:, :], ACT.Identity, bias=cols[:, 4:5]).then_inc(q_made, 1)

            act.wait_ge(setup_ev, 4)
            take_q(1)

            def exp_chunk(kind, g, q, c):
                p = g * GP + q
                if c == 0:
                    act.wait_ge(shifted, p + 1)
                    if not (kind == "first" and q == 0):
                        act.wait_ge(o1_made, p)
                s = S[:, c * SN:(c + 1) * SN]
                A(s, s, ACT.Exp, bias=nbias[:, 0:1], scale=SCALE, accum_out=rsum[:, c:c + 1]).then_inc(exped, 1)

            def copy_p(kind, g, q, c):
                p = g * GP + q
                act.wait_ge(p_turned, p * SC + c + 1)
                if not (kind == "first" and q == 0):
                    act.wait_ge(pv_done, p)
                if c < SC - 1:
                    copy(PT[:, c * 4:(c + 1) * 4, :].rearrange("p k t -> p (k t)"), SB_[c][:, :]).then_inc(p_copied, 1)
                else:
                    copy(PT[:, c * 4:KF, :].rearrange("p k t -> p (k t)"), SB_[c][:, 0:(KF - c * 4) * P])
                    copy(PT[0:KT, KF, :], SB_[c][0:KT, (KF - c * 4) * P:(KC - c * 4) * P]).then_inc(p_copied, 1)

            def take_o(g, q):
                act.wait_ge(o1_turned, g * GP + q)
                copy(o1T[:, :], MB[:, 0:P]).then_inc(o1T_made, 1)

            def take_x(g):
                act.wait_ge(xn_turned, g)
                A(xT[:, :].rearrange("p (c i) -> p c i", i=SQ),
                  MB[:, :].rearrange("p (c h) -> p c h", h=HALF)[:, :, 0:SQ], ACT.Copy, scale=cols[:, 3:4])\
                    .then_inc(xT_made, 1)

            def take_logits(g):
                act.wait_ge(routed, g)
                A(el[:, :, :].rearrange("p j e -> p (j e)"), MB[0:PT2, 0:GP * NE], ACT.Exp, scale=-1.0).then_inc(el_made, 1)

            def relu(g, n):
                f = g - 1
                if n < UNITS:
                    act.wait_ge(upped, f * UNITS + n + 1)
                    if n >= 2:
                        act.wait_ge(h_split, f * UNITS + n - 1)
                    A(Hf[:, n % 2, :], UB[n % 2][:, 0:GT], ACT.Relu, bias=b1[:, n:n + 1]).then_inc(relued, 1)
                if n - LAG == MC - 1:
                    act.wait_ge(downed, f * UNITS + MC)
                    copy(acc[:, :, :, 0:SQ].rearrange("p j b i -> p (j b) i"),
                         YB[:, 0:GT].rearrange("p (c i) -> p c i", i=SQ)).then_inc(y_read, 1)

            def body(kind, g):
                for q in range(GP):
                    sa, sb_ = steps_of(q)
                    attn, ffn, t = has(kind, "attn"), has(kind, "ffn"), has_tail(kind, q)
                    if t:
                        take_o(g, q)
                    chunks = list(range(SC)) if attn else []
                    if ffn:
                        for i, n in enumerate(sa):
                            relu(g, n)
                            if i >= 1 and chunks:
                                exp_chunk(kind, g, q, chunks.pop(0))
                    for c in chunks:
                        exp_chunk(kind, g, q, c)
                    if attn:
                        for c in range(SC):
                            copy_p(kind, g, q, c)
                    if ffn:
                        if q == 0:
                            take_x(g)
                            take_logits(g)
                        for n in sb_:
                            relu(g, n)
                    if q == GP - 1 and has(kind, "next_q"):
                        take_q(g + 2)

            run_bodies(act, body)

        @block.vector
        def _(dve):
            V = nc.vector
            made, before = [0], [0]

            stood = [0]

            def stand(sem, value):
                dve.wait_ge(sem, value)
                if not isinstance(value, int):
                    V.memset(scrap[:, stood[0]:stood[0] + 1], 0.0)
                    stood[0] += 1

            def own(ins, wait=dve.wait_ge):
                ins.then_inc(dve_step, 1)
                made[0] += 1
                wait(dve_step, before[0] + made[0])

            dve.wait_ge(mask_in, 16)
            V.tensor_scalar(mf, mi, 0.0, MASKED, ALU.is_equal, ALU.mult).then_inc(mbias_made, 1)
            V.memset(zero_pp, 0.0).then_inc(dve_init, 1)
            V.memset(acc[:, :, :, :], 0.0).then_inc(out_made, 1)
            V.memset(combT[:, :], 1.0)
            dve.wait_ge(small_in, SMALL)
            dve.wait_ge(dve_init, 1)
            V.tensor_scalar(bv_rep, zero_pp, cols[:, 2:3], None, ALU.add).then_inc(dve_init, 1)
            V.tensor_scalar(bq_rep, zero_pp, cols[:, 0:1], None, ALU.add).then_inc(dve_init, 1)

            def x0_stats(g):
                for j in range(GP):
                    i = V.bn_stats(st0[:, j, :], pair_of(X, g * GP + j))
                own(i, wait=stand)
                for j in range(GP):
                    i = V.bn_aggr(mv0[:, j, :], st0[:, j, :])
                own(i)
                V.tensor_scalar(ve0[:, :], mv0[:, :, 1], LN_EPS, None, ALU.add).then_inc(x0_stat, 1)

            def x0_normalise(g):
                dve.wait_ge(x0_rstd, g + 1)
                for j in range(GP):
                    i = V.tensor_scalar(xn0[:, j, :], pair_of(X, g * GP + j), mv0[:, j, 0:1], rs0[:, j:j + 1],
                                        ALU.subtract, ALU.mult)
                i.then_inc(x0_norm, 1)

            def take_c(g1):
                dve.wait_ge(c_projected, g1)
                V.tensor_scalar(cq[:, :], MB[:, 0:GP], cols[:, 6:7], None, ALU.add).then_inc(cq_made, 1)

            x0_stats(0)
            x0_normalise(0)
            dve.wait_ge(setup_ev, 4)
            V.tensor_tensor(bvo_bc[:, :], bvo_bc[:, :], bo_bc, ALU.add).then_inc(dve_init, 1)
            take_c(1)

            def mask_chunk(kind, g, q, c):
                p, slot = g * GP + q, q % 2
                if c == 0:
                    dve.wait_ge(mb_here[slot], 32 * (g * (GP // 2) + q // 2 + 1))
                    if kind == "first" and q == 0:
                        pass
                    else:
                        dve.wait_ge(p_turned, p * SC)
                stand(scored, p * SC + c + 1)
                V.tensor_tensor_reduce(out=S[:, c * SN:(c + 1) * SN], in0=SB_[c][:, 0:SN],
                                       in1=mb[:, slot, c * SN:(c + 1) * SN], scale=1.0, scalar=-3.0e38,
                                       op0=ALU.add, op1=ALU.max, accum_out=pmax[:, c:c + 1]).then_inc(masked, 1)

            def shift(g, q):
                p = g * GP + q
                dve.wait_ge(masked, (p + 1) * SC)
                own(V.tensor_reduce(mfull[:, :], pmax[:, :], AX.X, ALU.max))
                if q == 0:
                    dve.wait_ge(cq_made, g + 1)
                own(V.tensor_scalar(mc[:, :], mfull[:, :], cq[:, q:q + 1], None, ALU.add))
                V.tensor_scalar(nbias[:, :], cq[:, q:q + 1], mc[:, 0:1], SCALE, ALU.subtract, ALU.mult)\
                    .then_inc(shifted, 1)

            def make_o1(g, q):
                p1 = g * GP + q
                dve.wait_ge(exped, p1 * SC)
                own(V.tensor_reduce(rtot[:, :], rsum[:, :], AX.X, ALU.add))
                own(V.reciprocal(rinv[:, :], rtot[:, :]))
                dve.wait_ge(pv_done, p1)
                V.tensor_scalar(o1[:, :], OB[:, 0:D], rinv[:, 0:1], None, ALU.mult).then_inc(o1_made, 1)

            def tail1(kind, g, q):
                p1 = g * GP + q
                dve.wait_ge(projected, p1)
                if kind == "first" and q == 1:
                    dve.wait_ge(dve_init, 4)
                V.tensor_tensor(a1, MB[:, 0:D], bvo_bc[:, :], ALU.add).then_inc(a1_made, 1)
                dve.wait_ge(a1_made, p1)
                own(V.bn_stats(st1[:, :], a1), wait=stand)
                own(V.bn_aggr(mv1[:, :], st1[:, :]))
                V.tensor_scalar(ve1[:, :], mv1[:, 1:2], LN_EPS, None, ALU.add).then_inc(a_stat, 1)

            def tail2(g, q):
                dve.wait_ge(a_rstd, g * GP + q)
                V.tensor_scalar(a2, a1, mv1[:, 0:1], rs1[:, 0:1], ALU.subtract, ALU.mult).then_inc(a_norm, 1)

            def tail3(g, q):
                p1 = g * GP + q
                dve.wait_ge(x1_made, p1)
                own(V.bn_stats(st2[:, :], pair_of(X, p1 - 1)), wait=stand)
                own(V.bn_aggr(mv2[:, :], st2[:, :]))
                V.tensor_scalar(ve2[:, :], mv2[:, 1:2], 1.0 + RMS_EPS, LN_EPS * RMS_EPS, ALU.mult, ALU.add)\
                    .then_inc(x1_stat, 1)

            def tail4(g, q):
                p1 = g * GP + q
                dve.wait_ge(x1_rstd, p1)
                V.tensor_scalar(xn[:, (q - 1) % GP, :], pair_of(X, p1 - 1), mv2[:, 0:1], rs2[:, 0:1],
                                ALU.subtract, ALU.mult).then_inc(xn_made, 1)

            def split_x(g):
                dve.wait_ge(xT_made, g)
                V.tensor_copy(xh[:, :], xT[:, :]).then_inc(x_split, 1)
                dve.wait_ge(x_split, 2 * g - 1)
                V.tensor_tensor(xl[:, :], xT[:, :], xh[:, :].bitcast(F32), ALU.subtract).then_inc(x_split, 1)

            def combine(g):
                dve.wait_ge(el_made, g)
                own(V.tensor_scalar(el1[:, :, :], el[:, :, :], 1.0, None, ALU.add))
                own(V.reciprocal(pr[:, :, :], el1[:, :, :]))
                dve.wait_ge(pool_init, 3)
                for j in range(GP):
                    pj = pr[:, j, :].rearrange("p (o e) -> p o e", o=1).broadcast_to([PT2, NE, NE])
                    pe_ = pr[:, j, :].rearrange("p (e o) -> p e o", o=1).broadcast_to([PT2, NE, NE])
                    V.tensor_tensor(cmpg[:, j, :, :], pj, pe_, ALU.is_gt)
                    i = V.tensor_tensor(cmpe[:, j, :, :], pj, pe_, ALU.is_equal)
                own(i)
                lower = low[:, :, :].rearrange("p (o e) j -> p o e j", o=1).broadcast_to([PT2, GP, NE, NE])
                own(V.tensor_tensor(cmpe[:, :, :, :], cmpe[:, :, :, :], lower, ALU.mult))
                own(V.tensor_tensor(cmpg[:, :, :, :], cmpg[:, :, :, :], cmpe[:, :, :, :], ALU.add))
                own(V.tensor_reduce(rank[:, :, :], cmpg[:, :, :, :], AX.X, ALU.add))
                own(V.scalar_tensor_tensor(out=selp[:, :, :], in0=rank[:, :, :], scalar=1.5, in1=pr[:, :, :],
                                           op0=ALU.is_lt, op1=ALU.mult))
                own(V.tensor_reduce(ssum[:, :], selp[:, :, :], AX.X, ALU.add))
                own(V.tensor_scalar(sden[:, :], ssum[:, :], 1e-6, None, ALU.add))
                own(V.reciprocal(sinv[:, :], sden[:, :]))
                for j in range(GP):
                    i = V.tensor_scalar(comb[:, j, :], selp[:, j, :], sinv[:, j:j + 1], None, ALU.mult)
                i.then_inc(comb_made, 1)

            def take_comb(kind, g):
                dve.wait_ge(comb_turned, g)
                V.tensor_copy(combT[0:NE, :], MB[0:NE, 0:GT]).then_inc(combT_made, 1)

            def split_h(g, n):
                f, r = g - 1, n % HR
                if n < UNITS:
                    dve.wait_ge(relued, f * UNITS + n + 1)
                    if n >= HR:
                        dve.wait_ge(downed, f * UNITS + n - HR + 1)
                    V.tensor_copy(Hh[:, r, :], Hf[:, n % 2, :]).then_inc(h_hi, 1)
                    dve.wait_ge(h_hi, f * UNITS + n + 1)
                    V.tensor_tensor(Hl[:, r, :], Hf[:, n % 2, :], Hh[:, r, :].bitcast(F32), ALU.subtract)\
                        .then_inc(h_split, 1)
                e, m = (n - LAG) // MC, (n - LAG) % MC
                if m == MC - 1 and e >= 1:
                    if e == 1:
                        dve.wait_ge(comb_here, 16 * g)
                    if e >= 3:
                        dve.wait_ge(acc_added, f * NE + e - 2)
                    dve.wait_ge(downed, f * UNITS + n - LAG + 1)
                    V.tensor_tensor(tmp[:, e % 2, :], YB[:, 0:GT], comb_bc[:, (e - 1) * GT:e * GT], ALU.mult)\
                        .then_inc(y_read, 1)

            def finish(g):
                dve.wait_ge(y_turned, g)
                xg = X[:, bass.ds((g - 1) * GP, GP), :].rearrange("p j d -> p (j d)")
                V.tensor_tensor(xg, MB[:, :], xg, ALU.add).then_inc(out_made, 1)

            def body(kind, g):
                for q in range(GP):
                    sa, sb_ = steps_of(q)
                    attn, ffn, t = has(kind, "attn"), has(kind, "ffn"), has_tail(kind, q)
                    if t:
                        make_o1(g, q)
                    if q == 1 and ffn:
                        take_comb(kind, g)
                    front = []
                    if attn:
                        front = [lambda c=c: mask_chunk(kind, g, q, c) for c in range(SC)] + [lambda: shift(g, q)]
                    back = []
                    if t:
                        back = [lambda: tail1(kind, g, q), lambda: tail2(g, q), lambda: tail3(g, q), lambda: tail4(g, q)]
                    if q == 2 and has(kind, "next_q"):
                        back += [lambda: x0_stats(g + 1), lambda: x0_normalise(g + 1)]
                    for i, n in enumerate(sa if ffn else []):
                        for d in front[2 * i:2 * i + 2]:
                            d()
                        split_h(g, n)
                    for d in front[2 * len(sa) if ffn else 0:]:
                        d()
                    if q == 0 or not ffn:
                        for d in back:
                            d()
                        back = []
                        if ffn:
                            split_x(g)
                    for i, n in enumerate(sb_ if ffn else []):
                        if i < len(back):
                            back[i]()
                        split_h(g, n)
                    for d in back[len(sb_) if ffn else 0:]:
                        d()
                    if q == 0 and ffn:
                        combine(g)
                    if q == GP - 1 and has(kind, "next_q"):
                        take_c(g + 2)
                if ffn:
                    finish(g)

            body("first", 0)
            straight = made[0]
            with dve.Fori(1, GROUPS - 1) as g:
                before[0] = (g - 1) * OWN_MID
                body("mid", g)
            assert made[0] - straight == OWN_MID, made[0] - straight
            before[0] = (GROUPS - 3) * OWN_MID
            body("late", GROUPS - 1)
            body("last", GROUPS)


OWN_MID = 44

_INS = ['x', 'ctx_1024', 'ctxT', 'mask_Bx1xS2_ik1', 'WqT', 'L0_xattn_bq', 'WkT', 'L0_xattn_bk', 'WvT', 'L0_xattn_bv',
        'L0_xattn_Wo', 'L0_xattn_bo', 'L0_xattn_g0', 'L0_xattn_beta0', 'L0_ffn_norm_weight', 'router_wT',
        'L0_ffn_sw1', 'L0_ffn_sw2', 'L0_ffn_sb2', 'b1', 'L0_ffn_ew1', 'L0_ffn_ew2', 'L0_ffn_eb2', 'ident']


def kernel(**inputs):
    import numpy as np
    import concourse.bacc as bacc
    from concourse.bass_utils import run_bass_kernel_spmd

    a = {k: np.asarray(v) for k, v in inputs.items()}
    a['ctxT'] = a['ctx_1024'].transpose(0, 2, 1)
    a['WqT'] = a['L0_xattn_Wq'].T
    a['WkT'] = a['L0_xattn_Wk'].T
    a['WvT'] = a['L0_xattn_Wv'].T
    a['router_wT'] = a['L0_ffn_router_w'].T
    a['b1'] = np.concatenate([a['L0_ffn_sb1'].reshape(MC, P), a['L0_ffn_eb1'].reshape(NE * MC, P)]).T
    a['ident'] = np.eye(P, dtype=np.float32)
    nc = bacc.Bacc("TRN2", target_bir_lowering=False, num_devices=1)
    arrays, args = {}, []
    for name in _INS:
        v = np.ascontiguousarray(a[name])
        arrays[f"in_{name}_dram"] = v
        args.append(nc.dram_tensor(f"in_{name}_dram", v.shape, mybir.dt.from_np(v.dtype), kind="ExternalInput").ap())
    out = nc.dram_tensor("out_dram", (B, SQ, D), F32, kind="ExternalOutput").ap()
    build(nc, *args, out)
    r = run_bass_kernel_spmd(nc, [arrays], core_ids=[0])
    return r.results[0]["out_dram"]
```

```python
import concourse.bass as bass
from concourse import mybir
from contextlib import ExitStack

F32 = mybir.dt.float32
F32R = mybir.dt.float32r
BF16 = mybir.dt.bfloat16
I32 = mybir.dt.int32
ALU = mybir.AluOpType
ACT = mybir.ActivationFunctionType
AX = mybir.AxisListType

P = 128
B, SQ, D = 32, 56, 128
SK = 1500
HID = 512
NE = 8
NX = NE + 1
HALF = 64
PAIRS = B // 2
GP = 4
GROUPS = PAIRS // GP
GT = GP * 2 * SQ
PT2 = 2 * SQ
KC = (SK + P - 1) // P
KF = KC - 1
KT = SK - KF * P
SC = 3
SN = SK // SC
MC = HID // P
UNITS = NX * MC
LAG = 3
STEPS = UNITS + LAG
HR = 4
SCALE = 1.0 / float(D) ** 0.5
MASKED = -1.0e30
LN_EPS = 1e-5
RMS_EPS = 1e-8
PLAN = [(0, 4, 2), (5, 3, 3), (5, 3, 3), (5, 6, 0)]
assert sum(map(sum, PLAN)) == STEPS


def build(nc, x, ctx_in, ctxT_in, mask, mats_d, cols_d, rows_d, sw1, sw2, sb2, ew1, ew2, eb2, out):
    es = ExitStack()
    with es:
        def sb(name, shape, dt=F32):
            return es.enter_context(nc.sbuf_tensor(name, shape, dt))

        def ps(name, shape, dt=F32):
            return es.enter_context(nc.psum_tensor(name, shape, dt))

        def sem(name):
            return es.enter_context(nc.semaphore(name))

        mbias_d = nc.dram_tensor("mbias_scratch", [B, SK], BF16, kind="Internal").ap()
        comb_d = nc.dram_tensor("comb_scratch", [GROUPS, NE * GT], F32, kind="Internal").ap()

        mats = sb("mats_sb", [P, 5 * P])
        WqT_s, WkT_s, WvT_s, Wo_s, ident = (mats[:, i * P:(i + 1) * P] for i in range(5))
        rows = sb("rows_sb", [P, 3 * D])
        bo_bc, g0_bc, beta_bc = (rows[:, i * D:(i + 1) * D] for i in range(3))
        X = sb("X_sb", [P, PAIRS, D])
        ctxT = sb("ctxT_sb", [P, 2, 2, SK])
        ctxN = sb("ctxN_sb", [P, 2, 2, KC, D])
        mb = sb("mb_sb", [P, 2, SK], BF16)
        S = sb("S_sb", [P, SK])
        PT = sb("PT_sb", [P, KC, P])
        wh = sb("wh_sb", [P, NX, 2 * HID], F32R)
        wl = sb("wl_sb", [P, NX, 2 * HID], F32R)
        comb_bc = sb("comb_bc_sb", [P, NE * GT])
        qT = sb("qT_sb", [P, GP * P])
        xn0 = sb("xn0_sb", [P, GP, D])
        xn0T = sb("xn0T_sb", [P, GP * P])
        xn = sb("xn_sb", [P, GP, D])
        xT = sb("xT_sb", [P, GT])
        xh = sb("xh_sb", [P, GT], F32R)
        xl = sb("xl_sb", [P, GT], F32R)
        Hf = sb("Hf_sb", [P, 2, GT])
        Hh = sb("Hh_sb", [P, HR, GT], F32R)
        Hl = sb("Hl_sb", [P, HR, GT], F32R)
        acc = sb("acc_sb", [P, GP, 2, HALF])
        tmp = sb("tmp_sb", [P, 2, GT])
        o1 = sb("o1_sb", [P, D])
        o1T = sb("o1T_sb", [P, P])
        a1f = sb("a1f_sb", [P, 4 * D], BF16)
        a1 = a1f[:, 0:2 * D].bitcast(F32)
        a2 = a1f[:, 2 * D:4 * D].bitcast(F32)
        Wqk = sb("Wqk_sb", [P, D])
        Wvo = sb("Wvo_sb", [P, D])
        bv_rep, bq_rep, zero_pp = (tmp[:, 0, i * D:(i + 1) * D] for i in range(3))
        bv_wo = Hf[:, 0, 0:D]
        bvo_bc = sb("bvo_bc_sb", [P, D])
        prod = sb("prod_sb", [P, 3])
        cols = sb("cols_sb", [P, 4 + NE + UNITS])
        bq_c, bk_c, bv_c, nw_c = (cols[:, i:i + 1] for i in range(4))
        rwT = cols[:, 4:4 + NE]
        b1 = cols[:, 4 + NE:4 + NE + UNITS]
        b2 = sb("b2_sb", [NE + 1, D])
        combT = sb("combT_sb", [NE + 1, GP * 2, HALF])
        combJ = sb("combJ_sb", [GP * NE, PT2])
        mi = S[:, 0:B * SK // P].bitcast(I32)
        mf = a1f[:, 0:B * SK // P]
        mneg = sb("mneg_sb", [P, GP])
        low = sb("low_sb", [PT2, NE, NE])
        st0 = sb("st0_sb", [P, GP, 6])
        mv0 = sb("mv0_sb", [P, GP, 2])
        ve0 = sb("ve0_sb", [P, GP])
        rs0 = sb("rs0_sb", [P, GP])
        cq = sb("cq_sb", [P, GP])
        pmax = sb("pmax_sb", [P, SC])
        mfull = sb("mfull_sb", [P, 1])
        mc = sb("mc_sb", [P, 1])
        scrap = sb("scrap_sb", [1, 32])
        nbias = sb("nbias_sb", [P, 1])
        rsum = sb("rsum_sb", [P, SC])
        rtot = sb("rtot_sb", [P, 1])
        rinv = sb("rinv_sb", [P, 1])
        st1 = sb("st1_sb", [P, 6])
        mv1 = sb("mv1_sb", [P, 2])
        ve1 = sb("ve1_sb", [P, 1])
        rs1 = sb("rs1_sb", [P, 1])
        st2 = sb("st2_sb", [P, 6])
        mv2 = sb("mv2_sb", [P, 2])
        ve2 = sb("ve2_sb", [P, 1])
        rs2 = sb("rs2_sb", [P, 1])
        el = sb("el_sb", [PT2, GP, NE])
        pr = sb("pr_sb", [PT2, GP, NE])
        cmpg, cmpe = (tmp[0:PT2, i, 0:GP * NE * NE].rearrange("p (g e j) -> p g e j", g=GP, e=NE) for i in range(2))
        comb = sb("comb_sb", [PT2, GP, NE])
        rank = comb
        selp = sb("selp_sb", [PT2, GP, NE])
        ssum = sb("ssum_sb", [PT2, GP])
        sden = sb("sden_sb", [PT2, GP])
        sinv = sb("sinv_sb", [PT2, GP])

        SB_ = [ps(f"S{c}_ps", [P, 512]) for c in range(SC)]
        UB = [ps(f"U{c}_ps", [P, 512]) for c in range(2)]
        YB = [ps(f"Y{c}_ps", [P, 512]) for c in range(2)]
        MB = YB[1]
        OM = ps("O_ps", [P, 512])
        OB, AB, RB = OM[:, 0:D], OM[:, D:2 * D], OM[:, 2 * D:3 * D]

        mats_in = sem("mats_in")
        rows_in = sem("rows_in")
        x_in = sem("x_in")
        b2_here = sem("b2_here")
        x_rest_in = sem("x_rest_in")
        x_cleared = sem("x_cleared")
        mask_in = sem("mask_in")
        mbias_made = sem("mbias_made")
        mbias_out = sem("mbias_out")
        ctxT_here = [sem(f"ctxT_here{i}") for i in range(2)]
        ctxN_here = [sem(f"ctxN_here{i}") for i in range(2)]
        mb_here = [sem(f"mb_here{i}") for i in range(2)]
        w_here = [sem(f"w_here{i}") for i in range(3)]
        w_hi = sem("w_hi")
        w_split = sem("w_split")
        pool_init = sem("pool_init")
        dve_init = sem("dve_init")
        setup_mm = sem("setup_mm")
        setup_ev = sem("setup_ev")
        scored = sem("scored")
        masked = sem("masked")
        rsum_read = sem("rsum_read")
        shifted = sem("shifted")
        exped = sem("exped")
        p_turned = sem("p_turned")
        p_copied = sem("p_copied")
        pv_done = sem("pv_done")
        o1_made = sem("o1_made")
        o1_turned = sem("o1_turned")
        o1T_made = sem("o1T_made")
        projected = sem("projected")
        a1_made = sem("a1_made")
        xn_turned = sem("xn_turned")
        routed = sem("routed")
        comb_turned = sem("comb_turned")
        xn0_turned = sem("xn0_turned")
        xn0T_made = sem("xn0T_made")
        q_projected = sem("q_projected")
        q_made = sem("q_made")
        c_projected = sem("c_projected")
        y_turned = sem("y_turned")
        x0_stat = sem("x0_stat")
        x0_rstd = sem("x0_rstd")
        x0_norm = sem("x0_norm")
        xb_made = sem("xb_made")
        cq_made = sem("cq_made")
        a_stat = sem("a_stat")
        a_rstd = sem("a_rstd")
        x1_made = sem("x1_made")
        x1_stat = sem("x1_stat")
        x1_rstd = sem("x1_rstd")
        xn_made = sem("xn_made")
        xT_made = sem("xT_made")
        x_split = sem("x_split")
        el_made = sem("el_made")
        comb_made = sem("comb_made")
        combJ_made = sem("combJ_made")
        combT_clear = sem("combT_clear")
        combT_here = sem("combT_here")
        comb_out = sem("comb_out")
        comb_here = sem("comb_here")
        upped = sem("upped")
        relued = sem("relued")
        h_split = sem("h_split")
        downed = sem("downed")
        y_read = sem("y_read")
        acc_added = sem("acc_added")
        out_made = sem("out_made")
        out_sent = sem("out_sent")
        dve_step = sem("dve_step")

        def run_bodies(eng, body):
            body("first", 0)
            with eng.Fori(1, GROUPS - 1) as g:
                body("mid", g)
            body("late", GROUPS - 1)
            body("last", GROUPS)

        def has(kind, what):
            if what == "attn":
                return kind != "last"
            if what == "ffn":
                return kind != "first"
            if what == "next_q":
                return kind in ("first", "mid")

        def weighed_at(n):
            e, late = (n - LAG + 1) // MC - 1, (n - LAG + 1) % MC
            return e if e >= 1 and late == (2 if e == 1 else 0) else 0

        def raw_weights(e):
            return comb_bc[:, (e % 3) * 2 * HID:(e % 3 + 1) * 2 * HID]

        def thirds(q):
            return range((q - 1) * NX // 3, q * NX // 3) if q else ()

        def steps_of(q):
            n, out_ = sum(map(sum, PLAN[:q])), []
            for a in PLAN[q]:
                out_.append(list(range(n, n + a)))
                n += a
            return out_

        block = es.enter_context(nc.Block())

        def pair_in(sem_list, g, q, per, ahead=0):
            q += ahead
            return sem_list[q % 2], per * (g * (GP // 2) + q // 2 + 1)

        @block.sync
        def _(sp):
            def load_weights(third):
                if third:
                    sp.wait_ge(w_split, third * NX // 3)
                for e in range(third * NX // 3, (third + 1) * NX // 3):
                    s1, s2 = (sw1, sw2) if e == 0 else (ew1[e - 1], ew2[e - 1])
                    raw = raw_weights(e)
                    sp.dma_start(raw[:, 0:HID], s1).then_inc(w_here[third], 16)
                    sp.dma_start(raw[:, HID:2 * HID].rearrange("p (m d) -> p m d", m=MC),
                                 s2.rearrange("(m p) d -> p m d", m=MC)).then_inc(w_here[third], 16)

            def load_T(p, slot):
                sp.dma_start(ctxT[:, slot, :, :], ctxT_in[bass.ds(p * 2, 2), :, :].rearrange("b d k -> d b k"))\
                    .then_inc(ctxT_here[slot], 16)

            def load_mb(p, slot):
                for b in range(2):
                    sp.dma_start(mb[b * HALF:(b + 1) * HALF, slot, :],
                                 mbias_d[bass.ds(p * 2 + b, 1), :].broadcast_to([HALF, SK]))\
                        .then_inc(mb_here[slot], 16)

            def load_N(p, slot):
                src = ctx_in[bass.ds(p * 2, 2), :, :]
                sp.dma_start(ctxN[:, slot, :, 0:KF, :],
                             src[:, 0:KF * P, :].rearrange("b (k c) d -> k b c d", c=KF)).then_inc(ctxN_here[slot], 16)
                sp.dma_start(ctxN[0:KT, slot, :, KF, :],
                             src[:, KF * P:SK, :].rearrange("b k d -> k b d")).then_inc(ctxN_here[slot], 16)

            sp.dma_start(mi, mask.rearrange("b o k -> (b o k)").rearrange("(p n) -> p n", p=P)).then_inc(mask_in, 16)
            sp.dma_start(mats[:, :], mats_d).then_inc(mats_in, 16)
            sp.dma_start(cols[:, :], cols_d).then_inc(mats_in, 16)
            xv = x.rearrange("(p b) i d -> b i p d", b=2)
            sp.wait_ge(x_cleared, 1)
            for b in range(2):
                sp.dma_start(X[b * HALF:b * HALF + SQ, 0:GP, :], xv[b][:, 0:GP, :]).then_inc(x_in, 16)
            load_T(0, 0)
            sp.wait_ge(mbias_made, 1)
            sp.dma_start(mbias_d.rearrange("b k -> (b k)").rearrange("(p n) -> p n", p=P), mf).then_inc(mbias_out, 16)
            sp.dma_start(rows[:, :], rows_d.rearrange("(o d) -> o d", o=1).broadcast_to([P, 3 * D])).then_inc(rows_in, 16)
            sp.wait_ge(x_cleared, 2)
            sp.wait_ge(mbias_out, 16)
            load_mb(0, 0)
            load_N(0, 0)
            load_T(1, 1)
            load_mb(1, 1)
            for b in range(2):
                sp.dma_start(X[b * HALF:b * HALF + SQ, GP:PAIRS, :], xv[b][:, GP:PAIRS, :]).then_inc(x_rest_in, 16)
            load_N(1, 1)
            load_weights(0)
            sp.wait_ge(combT_clear, 1)
            sp.dma_start(b2[0:NE, :], eb2).then_inc(b2_here, 16)
            sp.dma_start(b2[NE:NE + 1, :], sb2.rearrange("(o d) -> o d", o=1)).then_inc(b2_here, 16)

            def body(kind, g):
                for q in range(GP):
                    p = g * GP + q
                    more = has(kind, "attn") and not (kind == "late" and q >= 2)
                    if more:
                        sp.wait_ge(scored, (p + 1) * SC)
                        load_T(p + 2, q % 2)
                        sp.wait_ge(masked, (p + 1) * SC)
                        load_mb(p + 2, q % 2)
                    if kind == "first" and 1 <= q < 3:
                        load_weights(q)
                    if q == 1 and has(kind, "ffn"):
                        f = g - 1
                        sp.wait_ge(combJ_made, g)
                        for j in range(GP):
                            sp.dma_start(comb_d[bass.ds(f, 1), :]
                                         .rearrange("o (e j t) -> j (o e) t", e=NE, j=GP)[j],
                                         combJ[j * NE:(j + 1) * NE, :]).then_inc(comb_out, 16)
                        sp.wait_ge(comb_out, g * GP * 16)
                        sp.dma_start(comb_bc[:, :], comb_d[bass.ds(f, 1), :].broadcast_to([P, NE * GT]))\
                            .then_inc(comb_here, 16)
                        sp.dma_start(combT[0:NE, :, 0:SQ], comb_d[bass.ds(f, 1), :]
                                     .rearrange("o (e c i) -> (o e) c i", e=NE, i=SQ)).then_inc(combT_here, 16)
                    if more:
                        sp.wait_ge(pv_done, p + 1)
                        load_N(p + 2, q % 2)

            run_bodies(sp, body)

        ov = out.rearrange("(p b) i d -> b i p d", b=2)

        def has_before(kind, q):
            return q > 0 and has(kind, "attn")

        def pair_of(t, p):
            return t[:, bass.ds(p, 1), :].rearrange("p o d -> p (o d)")

        @block.gpsimd
        def _(pool):
            pool.memset(X[:, 0:GP, :], 0.0).then_inc(x_cleared, 1)
            pool.memset(X[:, GP:PAIRS, :], 0.0).then_inc(x_cleared, 1)
            pool.memset(mneg[:, :], -0.5).then_inc(pool_init, 1)
            pool.memset(low[:, :, :], 1.0).then_inc(pool_init, 1)
            pool.wait_ge(pool_init, 2)
            pool.affine_select(out=low[:, :, :], in_=low[:, :, :], compare_op=ALU.is_ge, fill=0.0, base=-1,
                               pattern=[[1, NE], [-1, NE]], channel_multiplier=0).then_inc(pool_init, 1)

            def next_x(g, at):
                pool.wait_ge(x0_stat, at)
                pool.tensor_tensor(rs0[:, :], ve0[:, :], mneg[:, :], ALU.pow).then_inc(x0_rstd, 1)
                pool.wait_ge(x0_norm, at)
                pool.wait_ge(rows_in, 16)
                for j in range(GP):
                    xj = pair_of(X, g * GP + j)
                    pool.tensor_tensor(xj, xj, beta_bc[:, :], ALU.add).then_inc(xb_made, 1)

            next_x(0, 1)

            def rstds(kind, g, q):
                p1 = g * GP + q
                pool.wait_ge(a_stat, p1)
                pool.tensor_tensor(rs1[:, :], ve1[:, :], mneg[:, 0:1], ALU.pow).then_inc(a_rstd, 1)
                pool.wait_ge(x1_stat, p1)
                pool.tensor_tensor(rs2[:, :], ve2[:, :], mneg[:, 0:1], ALU.pow).then_inc(x1_rstd, 1)

            def add_expert(g, e):
                f = g - 1
                pool.wait_ge(y_read, f * NX + e + 1)
                if e > 1:
                    pool.wait_ge(acc_added, f * NE + e - 1)
                a = acc[:, :, :, 0:SQ].rearrange("p j b i -> p (j b) i")
                pool.tensor_tensor(a, a, tmp[:, e % 2, :].rearrange("p (c i) -> p c i", i=SQ), ALU.add)\
                    .then_inc(acc_added, 1)

            def body(kind, g):
                for q in range(GP):
                    if has_before(kind, q):
                        rstds(kind, g, q)
                    if q == 2 and has(kind, "next_q"):
                        next_x(g + 1, g + 2)
                    if has(kind, "ffn"):
                        for n in sum(steps_of(q), []):
                            if weighed_at(n):
                                add_expert(g, weighed_at(n))
                if has(kind, "attn"):
                    rstds(kind, g, GP)
                if has(kind, "ffn"):
                    f = g - 1
                    pool.wait_ge(out_made, g + 1)
                    for b in range(2):
                        pool.dma_start(ov[b][:, bass.ds(f * GP, GP), :],
                                       X[b * HALF:b * HALF + SQ, bass.ds(f * GP, GP), :]).then_inc(out_sent, 16)

            run_bodies(pool, body)
            pool.wait_ge(out_sent, GROUPS * 32)

        @block.tensor
        def _(pe):
            mm, tr = pe.matmul, pe.transpose

            pe.wait_ge(mats_in, 32)
            pe.wait_ge(dve_init, 3)
            mm(SB_[0][:, 0:D], WqT_s, WkT_s, start=True, stop=True).then_inc(setup_mm, 1)
            mm(UB[0][:, 0:1], WkT_s, bq_c, start=True, stop=True)
            mm(UB[0][:, 1:2], WqT_s, bk_c, start=True, stop=True)
            mm(UB[0][:, 2:3], bq_rep, bk_c, start=True, stop=True).then_inc(setup_mm, 1)
            mm(SB_[1][:, 0:D], WvT_s, Wo_s, start=True, stop=True).then_inc(setup_mm, 1)
            mm(SB_[2][:, 0:D], bv_rep, Wo_s, start=True, stop=True).then_inc(setup_mm, 1)

            def next_q(g1):
                pe.wait_ge(x0_norm, g1)
                if not isinstance(g1, int) or g1 > 2:
                    pe.wait_ge(y_read, (g1 - 3) * NX + 6)
                for j in range(GP):
                    last = tr(MB[:, j * P:(j + 1) * P], xn0[:, j, :], ident)
                last.then_inc(xn0_turned, 1)

            def next_q2(g1):
                pe.wait_ge(xn0T_made, g1)
                mm(MB[:, :], Wqk[:, :], xn0T[:, :], start=True, stop=True).then_inc(q_projected, 1)

            def next_c(g1):
                for j in range(GP):
                    last = mm(RB[:, j:j + 1], xn0T[:, j * P:(j + 1) * P], prod[:, 1:2], start=True, stop=True)
                last.then_inc(c_projected, 1)

            def scores(kind, g, q, ahead):
                qn = (q + ahead) % GP
                p = g * GP + q + ahead
                if qn == 0:
                    pe.wait_ge(q_made, g + 1 + ahead)
                pe.wait_ge(*pair_in(ctxT_here, g, q, 16, ahead))
                for c in range(SC):
                    if ahead:
                        pe.wait_ge(p_copied, (p - 1) * SC + c + 1)
                    for b in range(2):
                        last = mm(SB_[c][b * HALF:(b + 1) * HALF, 0:SN],
                                  qT[:, qn * P + b * HALF:qn * P + (b + 1) * HALF],
                                  ctxT[:, qn % 2, b, c * SN:(c + 1) * SN], start=True, stop=True)
                    last.then_inc(scored, 1)

            next_q(1)
            pe.wait_ge(setup_ev, 4)
            next_q2(1)
            next_c(1)
            scores("first", 0, 0, 0)

            def turn_p(g, q):
                p = g * GP + q
                pe.wait_ge(exped, (p + 1) * SC)
                for c in range(SC):
                    for i in range(4):
                        k = c * 4 + i
                        if k < KF:
                            last = tr(SB_[c][:, i * P:(i + 1) * P], S[:, k:KF * P:KF], ident)
                        else:
                            last = tr(SB_[c][0:KT, i * P:(i + 1) * P], S[:, KF * P:SK], ident)
                    last.then_inc(p_turned, 1)

            def pv(kind, g, q):
                p, slot = g * GP + q, q % 2
                pe.wait_ge(*pair_in(ctxN_here, g, q, 32))
                if not (kind == "first" and q == 0):
                    pe.wait_ge(a1_made, p)
                if q == 1 and has(kind, "ffn"):
                    pe.wait_ge(combJ_made, g)
                if q == GP - 1 and has(kind, "next_q"):
                    pe.wait_ge(cq_made, g + 2)
                for k in range(KC):
                    if k % 4 == 0:
                        pe.wait_ge(p_copied, p * SC + k // 4 + 1)
                    n = P if k < KF else KT
                    for b in range(2):
                        last = mm(OM[b * HALF:(b + 1) * HALF, 0:D], PT[0:n, k, b * HALF:(b + 1) * HALF],
                                  ctxN[0:n, slot, b, k, :], start=(k == 0), stop=(k == KC - 1))
                last.then_inc(pv_done, 1)

            def turn_o(kind, g, q):
                p1 = g * GP + q + 1
                pe.wait_ge(o1_made, p1)
                if q == 0 and has(kind, "ffn"):
                    pe.wait_ge(el_made, g)
                tr(AB, o1[:, :], ident).then_inc(o1_turned, 1)

            def proj(g, q):
                pe.wait_ge(o1T_made, g * GP + q + 1)
                mm(AB, o1T[:, :], Wvo[:, :], start=True, stop=True).then_inc(projected, 1)

            def turn_x(g):
                pe.wait_ge(xn_made, g * GP)
                pe.wait_ge(out_made, g)
                for j in range(GP):
                    last = tr(MB[:, j * P:(j + 1) * P], xn[:, j, :], ident)
                last.then_inc(xn_turned, 1)

            def route(kind, g):
                pe.wait_ge(xT_made, g)
                if kind != "last":
                    pe.wait_ge(o1_made, g * GP + 1)
                for j in range(GP):
                    last = mm(RB[0:PT2, j * NE:(j + 1) * NE], xT[:, j * PT2:(j + 1) * PT2], rwT,
                              start=True, stop=True)
                last.then_inc(routed, 1)

            def turn_comb(kind, g):
                pe.wait_ge(comb_made, g)
                if kind != "last":
                    pe.wait_ge(a1_made, g * GP + 1)
                tr(RB[0:GP * NE, 0:PT2], comb[:, :, :].rearrange("p j e -> p (j e)"), ident[0:PT2, 0:PT2])\
                    .then_inc(comb_turned, 1)

            def step(g, n):
                f = g - 1
                if n < UNITS:
                    e, m = n // MC, n % MC
                    if n == 0:
                        pe.wait_ge(x_split, 2 * g)
                        pe.wait_ge(w_split, NX)
                    if n >= 2:
                        pe.wait_ge(relued, f * UNITS + n - 1)
                    u = UB[n % 2][:, 0:GT]
                    w1 = slice(m * P, (m + 1) * P)
                    mm(u, wh[:, e, w1], xh[:, :], start=True, stop=False)
                    mm(u, wh[:, e, w1], xl[:, :], start=False, stop=False)
                    mm(u, wl[:, e, w1], xh[:, :], start=False, stop=True).then_inc(upped, 1)
                u = n - LAG
                if u >= 0:
                    e, m, r = u // MC, u % MC, u % HR
                    if m == 0 and e > 1:
                        pe.wait_ge(y_read, f * NX + e - 1)
                    pe.wait_ge(h_split, f * UNITS + u + 1)
                    y = YB[e % 2][:, 0:GT]
                    w2 = slice(HID + m * D, HID + (m + 1) * D)
                    mm(y, wh[:, e, w2], Hh[:, r, :], start=(m == 0), stop=False)
                    mm(y, wh[:, e, w2], Hl[:, r, :], start=False, stop=False)
                    i = mm(y, wl[:, e, w2], Hh[:, r, :], start=False, stop=(m == MC - 1))
                    i.then_inc(downed, 1)

            def turn_y(kind, g):
                pe.wait_ge(combT_here, g * 16)
                pe.wait_ge(b2_here, 32)
                pe.wait_ge(acc_added, g * NE)
                for j in range(GP):
                    y = MB[:, j * P:(j + 1) * P]
                    mm(y, combT[:, 2 * j:2 * j + 2, :].rearrange("e b i -> e (b i)"), b2[:, :], start=True, stop=False)
                    last = mm(y, acc[:, j, :, :].rearrange("p b i -> p (b i)"), ident, start=False, stop=True)
                last.then_inc(y_turned, 1)

            def body(kind, g):
                attn, ffn = has(kind, "attn"), has(kind, "ffn")
                for q in range(GP):
                    sa, sb1, sb2_ = steps_of(q) if ffn else ([], [], [])
                    next_q_here = q == GP - 1 and has(kind, "next_q")
                    if attn:
                        turn_p(g, q)
                    if next_q_here:
                        next_q(g + 2)
                    for i, n in enumerate(sa):
                        if i == 1 and next_q_here:
                            next_q2(g + 2)
                            pe.wait_ge(a1_made, g * GP + q)
                            next_c(g + 2)
                        if i == 1 and q == 1:
                            turn_comb(kind, g)
                        if i == 3 and next_q_here:
                            pe.wait_ge(q_made, g + 2)
                        step(g, n)
                    if next_q_here and not sa:
                        next_q2(g + 2)
                        pe.wait_ge(a1_made, g * GP + q)
                        next_c(g + 2)
                    if attn and (q < GP - 1 or has(kind, "next_q")):
                        scores(kind, g, q, 1)
                    if q == 0 and ffn:
                        turn_x(g)
                    if attn:
                        pv(kind, g, q)
                    if q == 0 and ffn:
                        route(kind, g)
                    for n in sb1:
                        step(g, n)
                    if attn:
                        turn_o(kind, g, q)
                    for n in sb2_:
                        step(g, n)
                    if attn:
                        proj(g, q)
                if ffn:
                    turn_y(kind, g)

            run_bodies(pe, body)

        @block.scalar
        def _(act):
            A = nc.scalar.activation

            def copy(dst, src):
                return A(dst, src, ACT.Copy)

            act.wait_ge(setup_mm, 1)
            copy(Wqk[:, :], SB_[0][:, 0:D]).then_inc(setup_ev, 1)
            act.wait_ge(setup_mm, 2)
            copy(prod[:, :], UB[0][:, 0:3]).then_inc(setup_ev, 1)
            act.wait_ge(setup_mm, 3)
            copy(Wvo[:, :], SB_[1][:, 0:D]).then_inc(setup_ev, 1)
            act.wait_ge(setup_mm, 4)
            copy(bv_wo, SB_[2][:, 0:D]).then_inc(setup_ev, 1)

            def take_q(g1):
                act.wait_ge(xn0_turned, g1)
                copy(xn0T[:, :], MB[:, :]).then_inc(xn0T_made, 1)

            def take_q2(g1):
                act.wait_ge(q_projected, g1)
                A(qT[:, :], MB[:, :], ACT.Identity, bias=prod[:, 0:1]).then_inc(q_made, 1)

            act.wait_ge(setup_ev, 4)
            take_q(1)
            take_q2(1)

            def split_hi(e):
                act.wait_ge(w_here[e * 3 // NX], NX // 3 * 32)
                copy(wh[:, e, :], raw_weights(e)).then_inc(w_hi, 1)

            def exp_chunk(p, c):
                if c == 0:
                    act.wait_ge(shifted, p + 1)
                    if not (isinstance(p, int) and p == 0):
                        act.wait_ge(rsum_read, p)
                s = S[:, c * SN:(c + 1) * SN]
                A(s, s, ACT.Exp, bias=nbias[:, 0:1], scale=SCALE, accum_out=rsum[:, c:c + 1]).then_inc(exped, 1)

            def copy_p(kind, g, q, c):
                p = g * GP + q
                act.wait_ge(p_turned, p * SC + c + 1)
                if not (kind == "first" and q == 0):
                    act.wait_ge(pv_done, p)
                if c < SC - 1:
                    copy(PT[:, c * 4:(c + 1) * 4, :].rearrange("p k t -> p (k t)"), SB_[c][:, :]).then_inc(p_copied, 1)
                else:
                    copy(PT[:, c * 4:KF, :].rearrange("p k t -> p (k t)"), SB_[c][:, 0:(KF - c * 4) * P])
                    copy(PT[0:KT, KF, :], SB_[c][0:KT, (KF - c * 4) * P:(KC - c * 4) * P]).then_inc(p_copied, 1)

            def take_o(g, q):
                act.wait_ge(o1_turned, g * GP + q + 1)
                copy(o1T[:, :], AB).then_inc(o1T_made, 1)

            def take_x(g):
                act.wait_ge(xn_turned, g)
                A(xT[:, :].rearrange("p (c i) -> p c i", i=SQ),
                  MB[:, :].rearrange("p (c h) -> p c h", h=HALF)[:, :, 0:SQ], ACT.Copy, scale=nw_c)\
                    .then_inc(xT_made, 1)

            def take_logits(g):
                act.wait_ge(routed, g)
                A(el[:, :, :].rearrange("p j e -> p (j e)"), RB[0:PT2, 0:GP * NE], ACT.Exp, scale=-1.0).then_inc(el_made, 1)

            def relu(g, n):
                f, r = g - 1, n % HR
                if n < UNITS:
                    act.wait_ge(upped, f * UNITS + n + 1)
                    if n >= 2:
                        act.wait_ge(h_split, f * UNITS + n - 1)
                    if n >= HR:
                        act.wait_ge(downed, f * UNITS + n - HR + 1)
                    u = UB[n % 2][:, 0:GT]
                    A(Hh[:, r, :], u, ACT.Relu, bias=b1[:, n:n + 1])
                    A(Hf[:, n % 2, :], u, ACT.Relu, bias=b1[:, n:n + 1]).then_inc(relued, 1)
                if n - LAG == MC - 1:
                    act.wait_ge(downed, f * UNITS + MC)
                    copy(acc[:, :, :, 0:SQ].rearrange("p j b i -> p (j b) i"),
                         YB[0][:, 0:GT].rearrange("p (c i) -> p c i", i=SQ)).then_inc(y_read, 1)

            for c in range(SC):
                exp_chunk(0, c)

            def body(kind, g):
                attn, ffn = has(kind, "attn"), has(kind, "ffn")
                for q in range(GP):
                    sa, sb1, sb2_ = steps_of(q) if ffn else ([], [], [])
                    next_q_here = q == GP - 1 and has(kind, "next_q")
                    chunks = list(range(SC)) if attn and (q < GP - 1 or has(kind, "next_q")) else []
                    if attn:
                        for c in range(SC):
                            copy_p(kind, g, q, c)
                    if next_q_here:
                        take_q(g + 2)
                    for i, n in enumerate(sa):
                        if i == 1 and next_q_here:
                            take_q2(g + 2)
                        relu(g, n)
                    if next_q_here and not sa:
                        take_q2(g + 2)
                    if kind == "first":
                        for e in thirds(q):
                            split_hi(e)
                    if ffn and q == 0:
                        take_x(g)
                        take_logits(g)
                    for i, n in enumerate(sb1):
                        relu(g, n)
                        if i >= 1 and chunks:
                            exp_chunk(g * GP + q + 1, chunks.pop(0))
                    if not ffn:
                        for c in chunks:
                            exp_chunk(g * GP + q + 1, c)
                        chunks = []
                    if attn:
                        take_o(g, q)
                    for n in sb2_:
                        relu(g, n)
                        if chunks:
                            exp_chunk(g * GP + q + 1, chunks.pop(0))

            run_bodies(act, body)

        @block.vector
        def _(dve):
            V = nc.vector
            made, before = [0], [0]

            stood = [0]

            def stand(sem, value):
                dve.wait_ge(sem, value)
                if not isinstance(value, int):
                    V.memset(scrap[:, stood[0]:stood[0] + 1], 0.0)
                    stood[0] += 1

            def own(ins, wait=dve.wait_ge):
                ins.then_inc(dve_step, 1)
                made[0] += 1
                wait(dve_step, before[0] + made[0])

            dve.wait_ge(mask_in, 16)
            V.tensor_scalar(mf, mi, 0.0, MASKED, ALU.is_equal, ALU.mult).then_inc(mbias_made, 1)
            V.memset(zero_pp, 0.0).then_inc(dve_init, 1)
            V.memset(acc[:, :, :, :], 0.0).then_inc(out_made, 1)
            V.memset(combT[:, :, :], 1.0).then_inc(combT_clear, 1)
            dve.wait_ge(mats_in, 32)
            dve.wait_ge(dve_init, 1)
            V.tensor_scalar(bv_rep, zero_pp, bv_c, None, ALU.add).then_inc(dve_init, 1)
            V.tensor_scalar(bq_rep, zero_pp, bq_c, None, ALU.add).then_inc(dve_init, 1)

            def x0_stats(g):
                for j in range(GP):
                    i = V.bn_stats(st0[:, j, :], pair_of(X, g * GP + j))
                own(i, wait=stand)
                for j in range(GP):
                    i = V.bn_aggr(mv0[:, j, :], st0[:, j, :])
                own(i)
                V.tensor_scalar(ve0[:, :], mv0[:, :, 1], LN_EPS, None, ALU.add).then_inc(x0_stat, 1)

            def x0_normalise(g):
                dve.wait_ge(x0_rstd, g + 1)
                for j in range(GP):
                    i = V.tensor_scalar(xn0[:, j, :], pair_of(X, g * GP + j), mv0[:, j, 0:1], rs0[:, j:j + 1],
                                        ALU.subtract, ALU.mult)
                i.then_inc(x0_norm, 1)

            def take_c(g1):
                dve.wait_ge(c_projected, g1)
                V.tensor_scalar(cq[:, :], RB[:, 0:GP], prod[:, 2:3], None, ALU.add).then_inc(cq_made, 1)

            dve.wait_ge(x_in, 32)
            x0_stats(0)
            x0_normalise(0)

            def mask_chunk(g, q, ahead, c):
                p, slot = g * GP + q + ahead, (q + ahead) % 2
                if c == 0:
                    dve.wait_ge(*pair_in(mb_here, g, q, 32, ahead))
                    if ahead:
                        dve.wait_ge(p_turned, p * SC)
                stand(scored, p * SC + c + 1)
                V.tensor_tensor_reduce(out=S[:, c * SN:(c + 1) * SN], in0=SB_[c][:, 0:SN],
                                       in1=mb[:, slot, c * SN:(c + 1) * SN], scale=1.0, scalar=-3.0e38,
                                       op0=ALU.add, op1=ALU.max, accum_out=pmax[:, c:c + 1]).then_inc(masked, 1)

            def shift(g, q, ahead):
                p, qn = g * GP + q + ahead, (q + ahead) % GP
                dve.wait_ge(masked, (p + 1) * SC)
                own(V.tensor_reduce(mfull[:, :], pmax[:, :], AX.X, ALU.max))
                if qn == 0:
                    dve.wait_ge(cq_made, g + 1 + ahead)
                own(V.tensor_scalar(mc[:, :], mfull[:, :], cq[:, qn:qn + 1], None, ALU.add))
                V.tensor_scalar(nbias[:, :], cq[:, qn:qn + 1], mc[:, 0:1], SCALE, ALU.subtract, ALU.mult)\
                    .then_inc(shifted, 1)

            def sum_rows(g, q):
                dve.wait_ge(exped, (g * GP + q + 1) * SC)
                V.tensor_reduce(rtot[:, :], rsum[:, :], AX.X, ALU.add).then_inc(rsum_read, 1)
                dve.wait_ge(rsum_read, g * GP + q + 1)
                own(V.reciprocal(rinv[:, :], rtot[:, :]))

            def make_o1(g, q):
                dve.wait_ge(pv_done, g * GP + q + 1)
                V.tensor_scalar(o1[:, :], OB, rinv[:, 0:1], None, ALU.mult).then_inc(o1_made, 1)

            def tail1(g, q):
                p1 = g * GP + q
                dve.wait_ge(projected, p1)
                V.tensor_tensor(a1, AB, bvo_bc[:, :], ALU.add).then_inc(a1_made, 1)
                dve.wait_ge(a1_made, p1)
                own(V.bn_stats(st1[:, :], a1), wait=stand)
                own(V.bn_aggr(mv1[:, :], st1[:, :]))
                V.tensor_scalar(ve1[:, :], mv1[:, 1:2], LN_EPS, None, ALU.add).then_inc(a_stat, 1)
                own(V.scalar_tensor_tensor(out=a2, in0=a1, scalar=mv1[:, 0:1], in1=g0_bc, op0=ALU.subtract, op1=ALU.mult))

            def tail2(g, q):
                p1 = g * GP + q
                dve.wait_ge(a_rstd, p1)
                dve.wait_ge(xb_made, p1)
                V.scalar_tensor_tensor(out=pair_of(X, p1 - 1), in0=a2, scalar=rs1[:, 0:1], in1=pair_of(X, p1 - 1),
                                       op0=ALU.mult, op1=ALU.add).then_inc(x1_made, 1)
                stand(x1_made, p1)
                own(V.bn_stats(st2[:, :], pair_of(X, p1 - 1)), wait=stand)
                own(V.bn_aggr(mv2[:, :], st2[:, :]))
                V.tensor_scalar(ve2[:, :], mv2[:, 1:2], 1.0 + RMS_EPS, LN_EPS * RMS_EPS, ALU.mult, ALU.add)\
                    .then_inc(x1_stat, 1)

            def tail3(g, q):
                p1 = g * GP + q
                dve.wait_ge(x1_rstd, p1)
                V.tensor_scalar(xn[:, (q - 1) % GP, :], pair_of(X, p1 - 1), mv2[:, 0:1], rs2[:, 0:1],
                                ALU.subtract, ALU.mult).then_inc(xn_made, 1)

            def split_lo(e):
                dve.wait_ge(w_hi, e + 1)
                V.tensor_tensor(wl[:, e, :], raw_weights(e),
                                wh[:, e, :].bitcast(F32), ALU.subtract).then_inc(w_split, 1)

            def split_x(g):
                dve.wait_ge(xT_made, g)
                V.tensor_copy(xh[:, :], xT[:, :]).then_inc(x_split, 1)
                dve.wait_ge(x_split, 2 * g - 1)
                V.tensor_tensor(xl[:, :], xT[:, :], xh[:, :].bitcast(F32), ALU.subtract).then_inc(x_split, 1)

            def combine(g):
                dve.wait_ge(el_made, g)
                own(V.tensor_scalar(el[:, :, :], el[:, :, :], 1.0, None, ALU.add))
                own(V.reciprocal(pr[:, :, :], el[:, :, :]))
                dve.wait_ge(pool_init, 3)
                for j in range(GP):
                    pj = pr[:, j, :].rearrange("p (o e) -> p o e", o=1).broadcast_to([PT2, NE, NE])
                    pe_ = pr[:, j, :].rearrange("p (e o) -> p e o", o=1).broadcast_to([PT2, NE, NE])
                    V.tensor_tensor(cmpg[:, j, :, :], pj, pe_, ALU.is_gt)
                    i = V.tensor_tensor(cmpe[:, j, :, :], pj, pe_, ALU.is_equal)
                own(i)
                lower = low[:, :, :].rearrange("p (o e) j -> p o e j", o=1).broadcast_to([PT2, GP, NE, NE])
                own(V.tensor_tensor(cmpe, cmpe, lower, ALU.mult))
                own(V.tensor_tensor(cmpg, cmpg, cmpe, ALU.add))
                own(V.tensor_reduce(rank[:, :, :], cmpg, AX.X, ALU.add))
                own(V.scalar_tensor_tensor(out=selp[:, :, :], in0=rank[:, :, :], scalar=1.5, in1=pr[:, :, :],
                                           op0=ALU.is_lt, op1=ALU.mult))
                own(V.tensor_reduce(ssum[:, :], selp[:, :, :], AX.X, ALU.add))
                own(V.tensor_scalar(sden[:, :], ssum[:, :], 1e-6, None, ALU.add))
                own(V.reciprocal(sinv[:, :], sden[:, :]))
                for j in range(GP):
                    i = V.tensor_scalar(comb[:, j, :], selp[:, j, :], sinv[:, j:j + 1], None, ALU.mult)
                i.then_inc(comb_made, 1)

            def take_comb(kind, g):
                dve.wait_ge(comb_turned, g)
                V.tensor_copy(combJ[:, :], RB[0:GP * NE, 0:PT2]).then_inc(combJ_made, 1)

            def split_h(g, n):
                f, r = g - 1, n % HR
                if n < UNITS:
                    dve.wait_ge(relued, f * UNITS + n + 1)
                    V.tensor_tensor(Hl[:, r, :], Hf[:, n % 2, :], Hh[:, r, :].bitcast(F32), ALU.subtract)\
                        .then_inc(h_split, 1)
                e = weighed_at(n)
                if e:
                    if e == 1:
                        dve.wait_ge(comb_here, 16 * g)
                    if e >= 3:
                        dve.wait_ge(acc_added, f * NE + e - 2)
                    dve.wait_ge(downed, f * UNITS + (e + 1) * MC)
                    V.tensor_tensor(tmp[:, e % 2, :], YB[e % 2][:, 0:GT], comb_bc[:, (e - 1) * GT:e * GT], ALU.mult)\
                        .then_inc(y_read, 1)

            def finish(g):
                dve.wait_ge(y_turned, g)
                xg = X[:, bass.ds((g - 1) * GP, GP), :].rearrange("p j d -> p (j d)")
                V.tensor_tensor(xg, MB[:, :], xg, ALU.add).then_inc(out_made, 1)

            take_c(1)
            for c in range(SC):
                mask_chunk(0, 0, 0, c)
            shift(0, 0, 0)
            dve.wait_ge(setup_ev, 4)
            dve.wait_ge(rows_in, 16)
            V.tensor_tensor(bvo_bc[:, :], bv_wo, bo_bc, ALU.add).then_inc(dve_init, 1)
            dve.wait_ge(dve_init, 4)
            dve.wait_ge(x_rest_in, 32)

            def body(kind, g):
                attn, ffn = has(kind, "attn"), has(kind, "ffn")
                for q in range(GP):
                    sa, sb1, sb2_ = steps_of(q) if ffn else ([], [], [])
                    scores_here = attn and (q < GP - 1 or has(kind, "next_q"))
                    back = []
                    if has_before(kind, q):
                        back = [lambda: tail1(g, q), lambda: tail2(g, q), lambda: tail3(g, q)]
                    if attn:
                        sum_rows(g, q)
                    if not ffn:
                        for d in back:
                            d()
                        back = []
                    if back:
                        back.pop(0)()
                    for i, n in enumerate(sa):
                        split_h(g, n)
                        if back:
                            back.pop(0)()
                        if i == 0 and q == 1:
                            take_comb(kind, g)
                        if i == 1 and q == GP - 1 and has(kind, "next_q"):
                            take_c(g + 2)
                    for d in back:
                        d()
                    if not sa and q == GP - 1 and has(kind, "next_q"):
                        take_c(g + 2)
                    if scores_here:
                        for c in range(SC):
                            mask_chunk(g, q, 1, c)
                        shift(g, q, 1)
                    if q == 0 and ffn:
                        split_x(g)
                    if attn:
                        make_o1(g, q)
                    if kind == "first":
                        for e in thirds(q):
                            split_lo(e)
                    for i, n in enumerate(sb1 + sb2_):
                        split_h(g, n)
                        if q == 0 and i == 1:
                            combine(g)
                        if q == 2 and has(kind, "next_q"):
                            if i == 1:
                                x0_stats(g + 1)
                            if i == 3:
                                x0_normalise(g + 1)
                    if q == 2 and has(kind, "next_q") and not ffn:
                        x0_stats(g + 1)
                        x0_normalise(g + 1)
                if attn:
                    tail1(g, GP)
                if ffn:
                    finish(g)
                if attn:
                    tail2(g, GP)
                    tail3(g, GP)

            body("first", 0)
            straight = made[0]
            with dve.Fori(1, GROUPS - 1) as g:
                before[0] = (g - 1) * OWN_MID
                body("mid", g)
            assert made[0] - straight == OWN_MID, made[0] - straight
            before[0] = (GROUPS - 3) * OWN_MID
            body("late", GROUPS - 1)
            body("last", GROUPS)


OWN_MID = 44

_INS = ['x', 'ctx_1024', 'ctxT', 'mask_Bx1xS2_ik1', 'mats', 'cols', 'rows', 'L0_ffn_sw1', 'L0_ffn_sw2',
        'L0_ffn_sb2', 'L0_ffn_ew1', 'L0_ffn_ew2', 'L0_ffn_eb2']


def kernel(**inputs):
    import numpy as np
    import concourse.bacc as bacc
    from concourse.bass_utils import run_bass_kernel_spmd

    a = {k: np.asarray(v) for k, v in inputs.items()}
    a['ctxT'] = a['ctx_1024'].transpose(0, 2, 1)
    a['mats'] = np.concatenate([a['L0_xattn_Wq'].T, a['L0_xattn_Wk'].T, a['L0_xattn_Wv'].T, a['L0_xattn_Wo'],
                                np.eye(P, dtype=np.float32)], axis=1)
    a['cols'] = np.concatenate([a['L0_xattn_bq'][:, None], a['L0_xattn_bk'][:, None], a['L0_xattn_bv'][:, None],
                                a['L0_ffn_norm_weight'][:, None], a['L0_ffn_router_w'].T,
                                a['L0_ffn_sb1'].reshape(MC, P).T, a['L0_ffn_eb1'].reshape(NE * MC, P).T], axis=1)
    a['rows'] = np.concatenate([a['L0_xattn_bo'], a['L0_xattn_g0'], a['L0_xattn_beta0']])
    nc = bacc.Bacc("TRN2", target_bir_lowering=False, num_devices=1)
    arrays, args = {}, []
    for name in _INS:
        v = np.ascontiguousarray(a[name])
        arrays[f"in_{name}_dram"] = v
        args.append(nc.dram_tensor(f"in_{name}_dram", v.shape, mybir.dt.from_np(v.dtype), kind="ExternalInput").ap())
    out = nc.dram_tensor("out_dram", (B, SQ, D), F32, kind="ExternalOutput").ap()
    build(nc, *args, out)
    r = run_bass_kernel_spmd(nc, [arrays], core_ids=[0])
    return r.results[0]["out_dram"]
```

```python
import concourse.bass as bass
from concourse import mybir
from contextlib import ExitStack

F32 = mybir.dt.float32
F32R = mybir.dt.float32r
BF16 = mybir.dt.bfloat16
I32 = mybir.dt.int32
ALU = mybir.AluOpType
ACT = mybir.ActivationFunctionType
AX = mybir.AxisListType

P = 128
B, SQ, D = 32, 56, 128
SK = 1500
HID = 512
NE = 8
NX = NE + 1
HALF = 64
PAIRS = B // 2
GP = 4
GROUPS = PAIRS // GP
GT = GP * 2 * SQ
PT2 = 2 * SQ
KC = (SK + P - 1) // P
KF = KC - 1
KT = SK - KF * P
SC = 3
SN = SK // SC
MC = HID // P
UNITS = NX * MC
LAG = 3
STEPS = UNITS + LAG
HR = 4
SCALE = 1.0 / float(D) ** 0.5
MASKED = -1.0e30
LN_EPS = 1e-5
RMS_EPS = 1e-8
PLAN = [(0, 3, 3), (5, 3, 3), (5, 3, 3), (5, 4, 2)]
assert sum(map(sum, PLAN)) == STEPS
FROM = [sum(map(sum, PLAN[:q])) for q in range(GP)]
IN_PV = [4, 8]
EXP_AFTER = 1
POOL_LO = [0, 1, 2]
DVE_HI = [3, 5] + [n for q in range(1, GP) for n in range(FROM[q] + PLAN[q][0] + 1, FROM[q] + PLAN[q][0] + 1 + SC)
                   if n < UNITS]


def build(nc, x, ctx_in, ctxT_in, mask, mats_d, cols_d, rows_d, sw1, sw2, sb2, ew1, ew2, eb2, out):
    es = ExitStack()
    with es:
        def sb(name, shape, dt=F32):
            return es.enter_context(nc.sbuf_tensor(name, shape, dt))

        def ps(name, shape, dt=F32):
            return es.enter_context(nc.psum_tensor(name, shape, dt))

        def sem(name):
            return es.enter_context(nc.semaphore(name))

        mbias_d = nc.dram_tensor("mbias_scratch", [B, SK], BF16, kind="Internal").ap()
        comb_d = nc.dram_tensor("comb_scratch", [GROUPS, NE * GT], F32, kind="Internal").ap()

        mats = sb("mats_sb", [P, 5 * P])
        WqT_s, WkT_s, WvT_s, Wo_s, ident = (mats[:, i * P:(i + 1) * P] for i in range(5))
        rows = sb("rows_sb", [P, 3 * D])
        bo_bc, g0_bc, beta_bc = (rows[:, i * D:(i + 1) * D] for i in range(3))
        X = sb("X_sb", [P, PAIRS, D])
        ctxT = sb("ctxT_sb", [P, 2, 2, SK])
        ctxN = sb("ctxN_sb", [P, 2, 2, KC, D])
        mb = sb("mb_sb", [P, 2, SK], BF16)
        S = sb("S_sb", [P, SK])
        PT = sb("PT_sb", [P, KC, P])
        wh = sb("wh_sb", [P, NX, 2 * HID], F32R)
        wl = sb("wl_sb", [P, NX, 2 * HID], F32R)
        comb_bc = sb("comb_bc_sb", [P, NE * GT])
        qT = sb("qT_sb", [P, GP * P])
        xn0 = sb("xn0_sb", [P, GP, D])
        xn0T = sb("xn0T_sb", [P, GP * P])
        y_last = xn0T[:, :].rearrange("p (c h) -> p c h", h=HALF)
        xn = sb("xn_sb", [P, GP, D])
        xT = sb("xT_sb", [P, GT])
        xh = sb("xh_sb", [P, GT], F32R)
        xl = sb("xl_sb", [P, GT], F32R)
        Hf = sb("Hf_sb", [P, 2, GT])
        Hh = sb("Hh_sb", [P, HR, GT], F32R)
        Hl = sb("Hl_sb", [P, HR, GT], F32R)
        acc = sb("acc_sb", [P, GP, 2, HALF])
        tmp = sb("tmp_sb", [P, 2, GT])
        o1 = sb("o1_sb", [P, D])
        o1T = sb("o1T_sb", [P, P])
        a1f = sb("a1f_sb", [P, 4 * D], BF16)
        a1 = a1f[:, 0:2 * D].bitcast(F32)
        a2 = a1f[:, 2 * D:4 * D].bitcast(F32)
        Wqk = sb("Wqk_sb", [P, D])
        Wvo = sb("Wvo_sb", [P, D])
        bv_rep, bq_rep, zero_pp = (tmp[:, 0, i * D:(i + 1) * D] for i in range(3))
        bv_wo = Hf[:, 0, 0:D]
        bvo_bc = sb("bvo_bc_sb", [P, D])
        prod = sb("prod_sb", [P, 3])
        cols = sb("cols_sb", [P, 4 + NE + UNITS])
        bq_c, bk_c, bv_c, nw_c = (cols[:, i:i + 1] for i in range(4))
        rwT = cols[:, 4:4 + NE]
        b1 = cols[:, 4 + NE:4 + NE + UNITS]
        b2 = sb("b2_sb", [NE + 1, D])
        combT = sb("combT_sb", [NE + 1, GP * 2, HALF])
        combJ = sb("combJ_sb", [NE * GP, PT2])
        mi = S[:, 0:B * SK // P].bitcast(I32)
        mf = a1f[:, 0:B * SK // P]
        mneg = sb("mneg_sb", [P, GP])
        low = sb("low_sb", [PT2, NE, NE])
        st0 = sb("st0_sb", [P, GP, 6])
        mv0 = sb("mv0_sb", [P, GP, 2])
        ve0 = sb("ve0_sb", [P, GP])
        rs0 = sb("rs0_sb", [P, GP])
        cq = sb("cq_sb", [P, GP])
        pmax = sb("pmax_sb", [P, SC])
        mfull = sb("mfull_sb", [P, 1])
        mc = sb("mc_sb", [P, 1])
        scrap = sb("scrap_sb", [1, 32])
        nbias = sb("nbias_sb", [P, 1])
        rsum = sb("rsum_sb", [P, SC])
        rtot = sb("rtot_sb", [P, 1])
        rinv = sb("rinv_sb", [P, 1])
        st1 = sb("st1_sb", [P, 6])
        mv1 = sb("mv1_sb", [P, 2])
        ve1 = sb("ve1_sb", [P, 1])
        rs1 = sb("rs1_sb", [P, 1])
        st2 = sb("st2_sb", [P, 6])
        mv2 = sb("mv2_sb", [P, 2])
        ve2 = sb("ve2_sb", [P, 1])
        rs2 = sb("rs2_sb", [P, 1])
        el = sb("el_sb", [PT2, GP, NE])
        pr = sb("pr_sb", [PT2, GP, NE])
        cmpg, cmpe = (tmp[0:PT2, i, 0:GP * NE * NE].rearrange("p (g e j) -> p g e j", g=GP, e=NE) for i in range(2))
        comb = sb("comb_sb", [PT2, NE, GP])
        rank = comb[:, :, :].rearrange("p e j -> p (e j)").rearrange("p (j e) -> p j e", e=NE)
        selp = sb("selp_sb", [PT2, GP, NE])
        ssum = sb("ssum_sb", [PT2, GP])
        sden = sb("sden_sb", [PT2, GP])
        sinv = sb("sinv_sb", [PT2, GP])

        SB_ = [ps(f"S{c}_ps", [P, 512]) for c in range(SC)]
        UB = [ps(f"U{c}_ps", [P, 512]) for c in range(2)]
        YB = [ps(f"Y{c}_ps", [P, 512]) for c in range(2)]
        MB = YB[1]
        OM = ps("O_ps", [P, 512])
        OB, AB, RB = OM[:, 0:D], OM[:, D:2 * D], OM[:, 2 * D:3 * D]

        mats_in = sem("mats_in")
        rows_in = sem("rows_in")
        x_in = sem("x_in")
        b2_here = sem("b2_here")
        x1_in = sem("x1_in")
        x_rest_in = sem("x_rest_in")
        x_cleared = sem("x_cleared")
        mask_in = sem("mask_in")
        mbias_made = sem("mbias_made")
        mbias_out = sem("mbias_out")
        ctxT_here = [sem(f"ctxT_here{i}") for i in range(2)]
        ctxN_here = [sem(f"ctxN_here{i}") for i in range(2)]
        mb_here = [sem(f"mb_here{i}") for i in range(2)]
        w_here = [sem(f"w_here{i}") for i in range(3)]
        w_hi = sem("w_hi")
        w_split = sem("w_split")
        pool_init = sem("pool_init")
        dve_init = sem("dve_init")
        setup_mm = sem("setup_mm")
        setup_ev = sem("setup_ev")
        scored = sem("scored")
        masked = sem("masked")
        rsum_read = sem("rsum_read")
        shifted = sem("shifted")
        exped = sem("exped")
        p_turned = sem("p_turned")
        p_copied = sem("p_copied")
        pv_done = sem("pv_done")
        o1_made = sem("o1_made")
        o1_turned = sem("o1_turned")
        o1T_made = sem("o1T_made")
        projected = sem("projected")
        a1_made = sem("a1_made")
        xn_turned = sem("xn_turned")
        routed = sem("routed")
        comb_turned = sem("comb_turned")
        xn0_turned = sem("xn0_turned")
        xn0T_made = sem("xn0T_made")
        q_projected = sem("q_projected")
        q_made = sem("q_made")
        c_projected = sem("c_projected")
        y_turned = sem("y_turned")
        x0_stat = sem("x0_stat")
        x0_rstd = sem("x0_rstd")
        x0_norm = sem("x0_norm")
        xb_made = sem("xb_made")
        cq_made = sem("cq_made")
        a_stat = sem("a_stat")
        a_rstd = sem("a_rstd")
        x1_made = sem("x1_made")
        x1_stat = sem("x1_stat")
        x1_rstd = sem("x1_rstd")
        xn_made = sem("xn_made")
        xT_made = sem("xT_made")
        x_hi = sem("x_hi")
        x_split = sem("x_split")
        el_made = sem("el_made")
        comb_made = sem("comb_made")
        combJ_made = sem("combJ_made")
        combT_clear = sem("combT_clear")
        combT_here = sem("combT_here")
        comb_out = sem("comb_out")
        comb_here = sem("comb_here")
        comb_rest_here = sem("comb_rest_here")
        upped = sem("upped")
        relued = sem("relued")
        h_split = sem("h_split")
        h_split_pool = sem("h_split_pool")
        h_hi = sem("h_hi")
        downed = sem("downed")
        y_read = sem("y_read")
        acc_added = sem("acc_added")
        out_made = sem("out_made")
        out_sent = sem("out_sent")
        dve_step = sem("dve_step")

        def run_bodies(eng, body):
            body("first", 0)
            with eng.Fori(1, GROUPS - 1) as g:
                body("mid", g)
            body("late", GROUPS - 1)
            body("last", GROUPS)

        def has(kind, what):
            if what == "attn":
                return kind != "last"
            if what == "ffn":
                return kind != "first"
            if what == "next_q":
                return kind in ("first", "mid")

        def hi_by_dve(n):
            return n in DVE_HI

        def lo_by_pool(n):
            return n in POOL_LO

        def hi_made(f, n):
            mine = [i for i in range(UNITS) if hi_by_dve(i)]
            return h_hi, f * len(mine) + mine.index(n) + 1

        def lo_made(f, n):
            before = sum(i <= n for i in POOL_LO)
            if lo_by_pool(n):
                return h_split_pool, f * len(POOL_LO) + before
            return h_split, f * (UNITS - len(POOL_LO)) + n + 1 - before

        def weighed_at(n):
            e, late = (n - LAG + 1) // MC - 1, (n - LAG + 1) % MC
            return e if e >= 1 and late == (2 if e == 1 else 0) else 0

        def raw_weights(e):
            return comb_bc[:, (e % 3) * 2 * HID:(e % 3 + 1) * 2 * HID]

        def thirds(q):
            k = {1: 0, 2: 1, GP: 2}.get(q)
            return [] if k is None else list(range(k * NX // 3, (k + 1) * NX // 3))

        def x_bank(kind):
            return SB_[0] if kind == "last" else MB

        def steps_of(q):
            n, out_ = FROM[q], []
            for a in PLAN[q]:
                out_.append(list(range(n, n + a)))
                n += a
            return out_

        block = es.enter_context(nc.Block())

        def pair_in(sem_list, g, q, per, ahead=0):
            q += ahead
            return sem_list[q % 2], per * (g * (GP // 2) + q // 2 + 1)

        @block.sync
        def _(sp):
            def load_weights(third):
                for e in range(third * NX // 3, (third + 1) * NX // 3):
                    s1, s2 = (sw1, sw2) if e == 0 else (ew1[e - 1], ew2[e - 1])
                    raw = raw_weights(e)
                    if e >= 3:
                        sp.wait_ge(w_split, e - 2)
                    sp.dma_start(raw[:, 0:HID], s1).then_inc(w_here[e % 3], 16)
                    sp.dma_start(raw[:, HID:2 * HID].rearrange("p (m d) -> p m d", m=MC),
                                 s2.rearrange("(m p) d -> p m d", m=MC)).then_inc(w_here[e % 3], 16)

            def load_x(g0, g1):
                sp.wait_ge(x_cleared, 2)
                for b in range(2):
                    sp.dma_start(X[b * HALF:b * HALF + SQ, g0 * GP:g1 * GP, :], xv[b][:, g0 * GP:g1 * GP, :])\
                        .then_inc(x1_in if g0 == 1 else x_rest_in, 16)

            def load_T(p, slot):
                sp.dma_start(ctxT[:, slot, :, :], ctxT_in[bass.ds(p * 2, 2), :, :].rearrange("b d k -> d b k"))\
                    .then_inc(ctxT_here[slot], 16)

            def load_mb(p, slot):
                for b in range(2):
                    sp.dma_start(mb[b * HALF:(b + 1) * HALF, slot, :],
                                 mbias_d[bass.ds(p * 2 + b, 1), :].broadcast_to([HALF, SK]))\
                        .then_inc(mb_here[slot], 16)

            def load_N(p, slot):
                src = ctx_in[bass.ds(p * 2, 2), :, :]
                sp.dma_start(ctxN[:, slot, :, 0:KF, :],
                             src[:, 0:KF * P, :].rearrange("b (k c) d -> k b c d", c=KF)).then_inc(ctxN_here[slot], 16)
                sp.dma_start(ctxN[0:KT, slot, :, KF, :],
                             src[:, KF * P:SK, :].rearrange("b k d -> k b d")).then_inc(ctxN_here[slot], 16)

            sp.dma_start(mi, mask.rearrange("b o k -> (b o k)").rearrange("(p n) -> p n", p=P)).then_inc(mask_in, 16)
            sp.dma_start(mats[:, :], mats_d).then_inc(mats_in, 16)
            sp.dma_start(cols[:, :], cols_d).then_inc(mats_in, 16)
            xv = x.rearrange("(p b) i d -> b i p d", b=2)
            ov = out.rearrange("(p b) i d -> b i p d", b=2)
            sp.wait_ge(x_cleared, 1)
            for b in range(2):
                sp.dma_start(X[b * HALF:b * HALF + SQ, 0:GP, :], xv[b][:, 0:GP, :]).then_inc(x_in, 16)
            load_T(0, 0)
            sp.wait_ge(mbias_made, 1)
            sp.dma_start(mbias_d.rearrange("b k -> (b k)").rearrange("(p n) -> p n", p=P), mf).then_inc(mbias_out, 16)
            sp.dma_start(rows[:, :], rows_d.rearrange("(o d) -> o d", o=1).broadcast_to([P, 3 * D])).then_inc(rows_in, 16)
            load_N(0, 0)
            sp.wait_ge(mbias_out, 16)
            load_mb(0, 0)
            load_T(1, 1)
            load_mb(1, 1)
            load_N(1, 1)
            def body(kind, g):
                for q in range(GP):
                    p = g * GP + q
                    more = has(kind, "attn") and not (kind == "late" and q >= 2)
                    if q == 1 and has(kind, "ffn"):
                        f = g - 1
                        sp.wait_ge(combJ_made, g)
                        sp.dma_start(comb_d[bass.ds(f, 1), :].rearrange("o (r t) -> (o r) t", t=PT2), combJ[:, :])\
                            .then_inc(comb_out, 16)
                        if kind == "mid":
                            sp.wait_ge(w_split, NX)
                        sp.wait_ge(comb_out, g * 16)
                        for part, here in ((slice(0, 2 * GT), comb_here), (slice(2 * GT, NE * GT), comb_rest_here)):
                            sp.dma_start(comb_bc[:, part], comb_d[bass.ds(f, 1), part]
                                         .broadcast_to([P, part.stop - part.start])).then_inc(here, 16)
                        sp.dma_start(combT[0:NE, :, 0:SQ], comb_d[bass.ds(f, 1), :]
                                     .rearrange("o (e c i) -> (o e) c i", e=NE, i=SQ)).then_inc(combT_here, 16)
                    if more:
                        sp.wait_ge(scored, (p + 1) * SC)
                        load_T(p + 2, q % 2)
                        sp.wait_ge(masked, (p + 1) * SC)
                        load_mb(p + 2, q % 2)
                    if kind == "first" and q == 0:
                        load_x(1, 2)
                    if kind == "first" and q < 3:
                        load_weights(q)
                    if kind == "first" and q == GP - 1:
                        sp.wait_ge(pv_done, p)
                        load_N(p + 1, (q + 1) % 2)
                    if more and not (kind == "first" and q == GP - 2):
                        sp.wait_ge(pv_done, p + 1)
                        load_N(p + 2, q % 2)
                if kind == "first":
                    load_x(2, GROUPS)
                    sp.wait_ge(combT_clear, 1)
                    sp.dma_start(b2[0:NE, :], eb2).then_inc(b2_here, 16)
                    sp.dma_start(b2[NE:NE + 1, :], sb2.rearrange("(o d) -> o d", o=1)).then_inc(b2_here, 16)
                if has(kind, "ffn"):
                    f = g - 1
                    sp.wait_ge(out_made, g + 1)
                    for b in range(2):
                        sp.dma_start(ov[b][:, bass.ds(f * GP, GP), :],
                                     X[b * HALF:b * HALF + SQ, bass.ds(f * GP, GP), :]).then_inc(out_sent, 16)

            run_bodies(sp, body)
            sp.wait_ge(out_sent, GROUPS * 32)

        def has_before(kind, q):
            return q > 0 and has(kind, "attn")

        def pair_of(t, p):
            return t[:, bass.ds(p, 1), :].rearrange("p o d -> p (o d)")

        @block.gpsimd
        def _(pool):
            pool.memset(X[:, 0:GP, :], 0.0).then_inc(x_cleared, 1)
            pool.memset(X[:, GP:PAIRS, :], 0.0).then_inc(x_cleared, 1)
            pool.memset(mneg[:, :], -0.5).then_inc(pool_init, 1)
            pool.memset(low[:, :, :], 1.0).then_inc(pool_init, 1)
            pool.wait_ge(pool_init, 2)
            pool.affine_select(out=low[:, :, :], in_=low[:, :, :], compare_op=ALU.is_ge, fill=0.0, base=-1,
                               pattern=[[1, NE], [-1, NE]], channel_multiplier=0).then_inc(pool_init, 1)

            def next_rstd(at):
                pool.wait_ge(x0_stat, at)
                pool.tensor_tensor(rs0[:, :], ve0[:, :], mneg[:, :], ALU.pow).then_inc(x0_rstd, 1)

            def next_x(g, at, pairs=range(GP)):
                pool.wait_ge(x0_norm, at)
                pool.wait_ge(rows_in, 16)
                for j in pairs:
                    xj = pair_of(X, g * GP + j)
                    pool.tensor_tensor(xj, xj, beta_bc[:, :], ALU.add).then_inc(xb_made, 1)

            next_rstd(1)
            next_x(0, 1)

            def split_lo(e):
                pool.wait_ge(w_hi, e + 1)
                pool.tensor_tensor(wl[:, e, :], raw_weights(e), wh[:, e, :].bitcast(F32), ALU.subtract)\
                    .then_inc(w_split, 1)

            def rstd1(g, q):
                p1 = g * GP + q
                pool.wait_ge(a_stat, p1)
                pool.tensor_tensor(rs1[:, :], ve1[:, :], mneg[:, 0:1], ALU.pow).then_inc(a_rstd, 1)

            def rstd2(g, q):
                p1 = g * GP + q
                pool.wait_ge(x1_stat, p1)
                pool.tensor_tensor(rs2[:, :], ve2[:, :], mneg[:, 0:1], ALU.pow).then_inc(x1_rstd, 1)

            def add_expert(g, e):
                f = g - 1
                pool.wait_ge(y_read, f * NX + e + 1)
                if e > 1:
                    pool.wait_ge(acc_added, f * (NE - 1) + e - 1)
                a = acc[:, :, :, 0:SQ].rearrange("p j b i -> p (j b) i")
                pool.tensor_tensor(a, a, tmp[:, e % 2, :].rearrange("p (c i) -> p c i", i=SQ), ALU.add)\
                    .then_inc(acc_added, 1)

            def body(kind, g):
                for q in range(GP):
                    if has_before(kind, q):
                        rstd1(g, q)
                        if kind == "first" and q == 2:
                            next_x(g + 1, g + 2)
                        if kind == "first":
                            for e in thirds(q)[0:2]:
                                split_lo(e)
                        if kind == "first" and q == 1:
                            next_rstd(g + 2)
                        rstd2(g, q)
                        if kind == "first":
                            for e in thirds(q)[2:3]:
                                split_lo(e)
                    if q == 2 and kind == "mid":
                        next_rstd(g + 2)
                    if has(kind, "ffn"):
                        for i, n in enumerate(sum(steps_of(q), [])):
                            if kind == "mid" and q == GP - 1 and i < GP:
                                next_x(g + 1, g + 2, [i])
                            if lo_by_pool(n):
                                pool.wait_ge(relued, (g - 1) * UNITS + n + 1)
                                if hi_by_dve(n):
                                    pool.wait_ge(*hi_made(g - 1, n))
                                pool.tensor_tensor(Hl[:, n % HR, :], Hf[:, n % 2, :], Hh[:, n % HR, :].bitcast(F32),
                                                   ALU.subtract).then_inc(h_split_pool, 1)
                            if 1 <= weighed_at(n) < NE:
                                add_expert(g, weighed_at(n))
                if has(kind, "attn"):
                    rstd1(g, GP)
                    rstd2(g, GP)
                if kind == "first":
                    for e in thirds(GP):
                        split_lo(e)

            run_bodies(pool, body)

        @block.tensor
        def _(pe):
            mm, tr = pe.matmul, pe.transpose

            pe.wait_ge(mats_in, 32)
            pe.wait_ge(dve_init, 3)
            mm(SB_[0][:, 0:D], WqT_s, WkT_s, start=True, stop=True).then_inc(setup_mm, 1)
            mm(UB[0][:, 0:1], WkT_s, bq_c, start=True, stop=True)
            mm(UB[0][:, 1:2], WqT_s, bk_c, start=True, stop=True)
            mm(UB[0][:, 2:3], bq_rep, bk_c, start=True, stop=True).then_inc(setup_mm, 1)
            mm(SB_[1][:, 0:D], WvT_s, Wo_s, start=True, stop=True).then_inc(setup_mm, 1)
            mm(SB_[2][:, 0:D], bv_rep, Wo_s, start=True, stop=True).then_inc(setup_mm, 1)

            def next_q(g1):
                pe.wait_ge(x0_norm, g1)
                if not isinstance(g1, int) or g1 > 2:
                    pe.wait_ge(y_read, (g1 - 3) * NX + 6)
                for j in range(GP):
                    last = tr(MB[:, j * P:(j + 1) * P], xn0[:, j, :], ident)
                last.then_inc(xn0_turned, 1)

            def next_q2(g1):
                pe.wait_ge(xn0T_made, g1)
                mm(MB[:, :], Wqk[:, :], xn0T[:, :], start=True, stop=True).then_inc(q_projected, 1)

            def next_c(g1):
                for j in range(GP):
                    last = mm(RB[:, j:j + 1], xn0T[:, j * P:(j + 1) * P], prod[:, 1:2], start=True, stop=True)
                last.then_inc(c_projected, 1)

            def turn_x(kind, g):
                pe.wait_ge(xn_made, g * GP)
                if kind != "last":
                    pe.wait_ge(out_made, g)
                for j in range(GP):
                    last = tr(x_bank(kind)[:, j * P:(j + 1) * P], xn[:, j, :], ident)
                last.then_inc(xn_turned, 1)

            def route(kind, g):
                pe.wait_ge(xT_made, g)
                for j in range(GP):
                    last = mm(x_bank(kind)[0:PT2, j * NE:(j + 1) * NE], xT[:, j * PT2:(j + 1) * PT2], rwT,
                              start=True, stop=True)
                last.then_inc(routed, 1)

            def scores(kind, g, q, ahead):
                qn = (q + ahead) % GP
                p = g * GP + q + ahead
                if qn == 0:
                    pe.wait_ge(q_made, g + 1 + ahead)
                pe.wait_ge(*pair_in(ctxT_here, g, q, 16, ahead))
                for c in range(SC):
                    if c == 1 and ahead and q == 0 and has(kind, "ffn"):
                        turn_x(kind, g)
                    if ahead:
                        pe.wait_ge(p_copied, (p - 1) * SC + c + 1)
                    for b in range(2):
                        last = mm(SB_[c][b * HALF:(b + 1) * HALF, 0:SN],
                                  qT[:, qn * P + b * HALF:qn * P + (b + 1) * HALF],
                                  ctxT[:, qn % 2, b, c * SN:(c + 1) * SN], start=True, stop=True)
                    last.then_inc(scored, 1)

            next_q(1)
            pe.wait_ge(setup_ev, 4)
            next_q2(1)
            next_c(1)
            scores("first", 0, 0, 0)

            def turn_p(g, q):
                p = g * GP + q
                pe.wait_ge(exped, (p + 1) * SC)
                for c in range(SC):
                    for i in range(4):
                        k = c * 4 + i
                        if k < KF:
                            last = tr(SB_[c][:, i * P:(i + 1) * P], S[:, k:KF * P:KF], ident)
                        else:
                            last = tr(SB_[c][0:KT, i * P:(i + 1) * P], S[:, KF * P:SK], ident)
                    last.then_inc(p_turned, 1)

            def step(g, n):
                f = g - 1
                if n < UNITS:
                    e, m = n // MC, n % MC
                    if n == 0:
                        pe.wait_ge(x_split, g)
                    if m == 0:
                        pe.wait_ge(w_split, e + 1)
                    if n >= 2:
                        pe.wait_ge(relued, f * UNITS + n - 1)
                    u = UB[n % 2][:, 0:GT]
                    w1 = slice(m * P, (m + 1) * P)
                    mm(u, wh[:, e, w1], xh[:, :], start=True, stop=False)
                    mm(u, wh[:, e, w1], xl[:, :], start=False, stop=False)
                    mm(u, wl[:, e, w1], xh[:, :], start=False, stop=True).then_inc(upped, 1)
                u = n - LAG
                if u >= 0:
                    e, m, r = u // MC, u % MC, u % HR
                    if m == 0 and e == 1:
                        pe.wait_ge(combJ_made, g)
                    if m == 0 and e > 1:
                        pe.wait_ge(y_read, f * NX + e - 1)
                    pe.wait_ge(*lo_made(f, u))
                    y = YB[e % 2][:, 0:GT]
                    w2 = slice(HID + m * D, HID + (m + 1) * D)
                    mm(y, wh[:, e, w2], Hh[:, r, :], start=(m == 0), stop=False)
                    mm(y, wh[:, e, w2], Hl[:, r, :], start=False, stop=False)
                    i = mm(y, wl[:, e, w2], Hh[:, r, :], start=False, stop=(m == MC - 1))
                    i.then_inc(downed, 1)

            def pv(kind, g, q):
                p, slot = g * GP + q, q % 2
                pe.wait_ge(*pair_in(ctxN_here, g, q, 32))
                if not (kind == "first" and q == 0):
                    pe.wait_ge(a1_made, p)
                if q == GP - 1 and has(kind, "next_q"):
                    pe.wait_ge(cq_made, g + 2)
                for k in range(KC):
                    if k in IN_PV and q == 0 and has(kind, "ffn"):
                        step(g, IN_PV.index(k))
                    if k % 4 == 0:
                        pe.wait_ge(p_copied, p * SC + k // 4 + 1)
                    n = P if k < KF else KT
                    for b in range(2):
                        last = mm(OM[b * HALF:(b + 1) * HALF, 0:D], PT[0:n, k, b * HALF:(b + 1) * HALF],
                                  ctxN[0:n, slot, b, k, :], start=(k == 0), stop=(k == KC - 1))
                last.then_inc(pv_done, 1)

            def turn_o(kind, g, q):
                p1 = g * GP + q + 1
                pe.wait_ge(o1_made, p1)
                tr(AB, o1[:, :], ident).then_inc(o1_turned, 1)

            def proj(g, q):
                pe.wait_ge(o1T_made, g * GP + q + 1)
                mm(AB, o1T[:, :], Wvo[:, :], start=True, stop=True).then_inc(projected, 1)

            def turn_comb(kind, g):
                pe.wait_ge(comb_made, g)
                if kind == "last":
                    pe.wait_ge(out_made, g)
                tr(MB[0:NE * GP, 0:PT2], comb[:, :, :].rearrange("p e j -> p (e j)"), ident[0:PT2, 0:PT2])\
                    .then_inc(comb_turned, 1)

            def turn_y(g):
                pe.wait_ge(combT_here, g * 16)
                pe.wait_ge(b2_here, 32)
                pe.wait_ge(acc_added, g * (NE - 1))
                for j in range(GP):
                    y = MB[:, j * P:(j + 1) * P]
                    mm(y, combT[:, 2 * j:2 * j + 2, :].rearrange("e b i -> e (b i)"), b2[:, :],
                       start=(j == 0), stop=False)
                    mm(y, acc[:, j, :, :].rearrange("p b i -> p (b i)"), ident, start=False, stop=False)
                pe.wait_ge(y_read, g * NX)
                for j in range(GP):
                    last = mm(MB[:, j * P:(j + 1) * P], xn0T[:, j * P:(j + 1) * P], ident,
                              start=False, stop=(j == GP - 1))
                last.then_inc(y_turned, 1)

            def body(kind, g):
                attn, ffn = has(kind, "attn"), has(kind, "ffn")
                for q in range(GP):
                    sa, sb1, sb2_ = steps_of(q) if ffn else ([], [], [])
                    next_q_here = q == GP - 1 and has(kind, "next_q") and kind != "first"
                    if attn:
                        turn_p(g, q)
                    if next_q_here:
                        next_q(g + 2)
                    for i, n in enumerate(sa):
                        if i == 1 and next_q_here:
                            next_q2(g + 2)
                            pe.wait_ge(a1_made, g * GP + q)
                            next_c(g + 2)
                        if i == 3 and next_q_here:
                            pe.wait_ge(q_made, g + 2)
                        step(g, n)
                    if kind == "first" and q == GP - 1:
                        pe.wait_ge(a1_made, g * GP + q)
                        next_c(g + 2)
                    if attn and (q < GP - 1 or has(kind, "next_q")):
                        scores(kind, g, q, 1)
                    if q == 0 and ffn:
                        if not attn:
                            turn_x(kind, g)
                        route(kind, g)
                    if attn:
                        pv(kind, g, q)
                    for n in sb1:
                        if not (n < len(IN_PV) and attn):
                            step(g, n)
                    if kind == "first" and q == GP - 2:
                        next_q(g + 2)
                    if attn:
                        turn_o(kind, g, q)
                    if kind == "first" and q == GP - 2:
                        next_q2(g + 2)
                    for n in sb2_:
                        step(g, n)
                    if q == 0 and ffn:
                        turn_comb(kind, g)
                    if attn:
                        proj(g, q)
                if ffn:
                    turn_y(g)

            run_bodies(pe, body)

        @block.scalar
        def _(act):
            A = nc.scalar.activation

            def copy(dst, src):
                return A(dst, src, ACT.Copy)

            act.wait_ge(setup_mm, 1)
            copy(Wqk[:, :], SB_[0][:, 0:D]).then_inc(setup_ev, 1)
            act.wait_ge(setup_mm, 2)
            copy(prod[:, :], UB[0][:, 0:3]).then_inc(setup_ev, 1)
            act.wait_ge(setup_mm, 3)
            copy(Wvo[:, :], SB_[1][:, 0:D]).then_inc(setup_ev, 1)
            act.wait_ge(setup_mm, 4)
            copy(bv_wo, SB_[2][:, 0:D]).then_inc(setup_ev, 1)

            def take_q(g1):
                act.wait_ge(xn0_turned, g1)
                copy(xn0T[:, :], MB[:, :]).then_inc(xn0T_made, 1)

            def take_q2(g1):
                act.wait_ge(q_projected, g1)
                A(qT[:, :], MB[:, :], ACT.Identity, bias=prod[:, 0:1]).then_inc(q_made, 1)

            act.wait_ge(setup_ev, 4)
            take_q(1)
            take_q2(1)

            def split_hi(e):
                act.wait_ge(w_here[e % 3], 32 * (e // 3 + 1))
                copy(wh[:, e, :], raw_weights(e)).then_inc(w_hi, 1)

            def exp_chunk(p, c):
                if c == 0:
                    act.wait_ge(shifted, p + 1)
                    if not (isinstance(p, int) and p == 0):
                        act.wait_ge(rsum_read, p)
                s = S[:, c * SN:(c + 1) * SN]
                A(s, s, ACT.Exp, bias=nbias[:, 0:1], scale=SCALE, accum_out=rsum[:, c:c + 1]).then_inc(exped, 1)

            def copy_p(kind, g, q, c):
                p = g * GP + q
                act.wait_ge(p_turned, p * SC + c + 1)
                if not (kind == "first" and q == 0):
                    act.wait_ge(pv_done, p)
                if c < SC - 1:
                    copy(PT[:, c * 4:(c + 1) * 4, :].rearrange("p k t -> p (k t)"), SB_[c][:, :]).then_inc(p_copied, 1)
                else:
                    copy(PT[:, c * 4:KF, :].rearrange("p k t -> p (k t)"), SB_[c][:, 0:(KF - c * 4) * P])
                    copy(PT[0:KT, KF, :], SB_[c][0:KT, (KF - c * 4) * P:(KC - c * 4) * P]).then_inc(p_copied, 1)

            def take_o(g, q):
                act.wait_ge(o1_turned, g * GP + q + 1)
                copy(o1T[:, :], AB).then_inc(o1T_made, 1)

            def take_x(kind, g):
                act.wait_ge(xn_turned, g)
                A(xT[:, :].rearrange("p (c i) -> p c i", i=SQ),
                  x_bank(kind)[:, :].rearrange("p (c h) -> p c h", h=HALF)[:, :, 0:SQ], ACT.Copy, scale=nw_c)\
                    .then_inc(xT_made, 1)
                act.wait_ge(xT_made, g)
                copy(xh[:, :], xT[:, :]).then_inc(x_hi, 1)

            def take_logits(kind, g):
                act.wait_ge(routed, g)
                A(el[:, :, :].rearrange("p j e -> p (j e)"), x_bank(kind)[0:PT2, 0:GP * NE], ACT.Exp, scale=-1.0)\
                    .then_inc(el_made, 1)

            def relu(g, n):
                f, r = g - 1, n % HR
                if n < UNITS:
                    act.wait_ge(upped, f * UNITS + n + 1)
                    if n >= 2:
                        act.wait_ge(*lo_made(f, n - 2))
                    if n >= HR:
                        act.wait_ge(downed, f * UNITS + n - HR + 1)
                    u = UB[n % 2][:, 0:GT]
                    if not hi_by_dve(n):
                        A(Hh[:, r, :], u, ACT.Relu, bias=b1[:, n:n + 1])
                    A(Hf[:, n % 2, :], u, ACT.Relu, bias=b1[:, n:n + 1]).then_inc(relued, 1)
                if n - LAG == MC - 1:
                    act.wait_ge(downed, f * UNITS + MC)
                    copy(acc[:, :, :, 0:SQ].rearrange("p j b i -> p (j b) i"),
                         YB[0][:, 0:GT].rearrange("p (c i) -> p c i", i=SQ)).then_inc(y_read, 1)

            for c in range(SC):
                exp_chunk(0, c)

            def body(kind, g):
                attn, ffn = has(kind, "attn"), has(kind, "ffn")
                for q in range(GP):
                    sa, sb1, sb2_ = steps_of(q) if ffn else ([], [], [])
                    next_q_here = q == GP - 1 and has(kind, "next_q") and kind != "first"
                    exps_here = attn and (q < GP - 1 or has(kind, "next_q"))
                    if attn:
                        for c in range(SC):
                            copy_p(kind, g, q, c)
                    if next_q_here:
                        take_q(g + 2)
                    for i, n in enumerate(sa):
                        if i == 1 and next_q_here:
                            take_q2(g + 2)
                        relu(g, n)
                    if kind == "first" and q < 3:
                        for e in thirds(q):
                            split_hi(e)
                    if ffn and q == 0:
                        take_x(kind, g)
                        take_logits(kind, g)
                    for i, n in enumerate(sb1):
                        relu(g, n)
                        if exps_here and 0 <= i - EXP_AFTER < SC:
                            exp_chunk(g * GP + q + 1, i - EXP_AFTER)
                    if exps_here and not ffn:
                        for c in range(SC):
                            exp_chunk(g * GP + q + 1, c)
                    if kind == "first" and q == GP - 2:
                        take_q(g + 2)
                    if attn:
                        take_o(g, q)
                    if kind == "first" and q == GP - 2:
                        take_q2(g + 2)
                    if kind == "first" and q == GP - 1:
                        for e in thirds(GP):
                            split_hi(e)
                    for i, n in enumerate(sb2_, len(sb1)):
                        relu(g, n)
                        if exps_here and 0 <= i - EXP_AFTER < SC:
                            exp_chunk(g * GP + q + 1, i - EXP_AFTER)

            run_bodies(act, body)

        @block.vector
        def _(dve):
            V = nc.vector
            made, before = [0], [0]

            stood = [0]

            def stand(sem, value):
                dve.wait_ge(sem, value)
                if not isinstance(value, int):
                    V.memset(scrap[:, stood[0]:stood[0] + 1], 0.0)
                    stood[0] += 1

            def own(ins, wait=dve.wait_ge):
                ins.then_inc(dve_step, 1)
                made[0] += 1
                wait(dve_step, before[0] + made[0])

            dve.wait_ge(mask_in, 16)
            V.tensor_scalar(mf, mi, 0.0, MASKED, ALU.is_equal, ALU.mult).then_inc(mbias_made, 1)
            V.memset(zero_pp, 0.0).then_inc(dve_init, 1)
            V.memset(acc[:, :, :, :], 0.0).then_inc(out_made, 1)
            V.memset(combT[:, :, :], 1.0).then_inc(combT_clear, 1)
            dve.wait_ge(mats_in, 32)
            dve.wait_ge(dve_init, 1)
            V.tensor_scalar(bv_rep, zero_pp, bv_c, None, ALU.add).then_inc(dve_init, 1)
            V.tensor_scalar(bq_rep, zero_pp, bq_c, None, ALU.add).then_inc(dve_init, 1)

            def x0_stats(g):
                for j in range(GP):
                    i = V.bn_stats(st0[:, j, :], pair_of(X, g * GP + j))
                own(i, wait=stand)
                for j in range(GP):
                    i = V.bn_aggr(mv0[:, j, :], st0[:, j, :])
                own(i)
                V.tensor_scalar(ve0[:, :], mv0[:, :, 1], LN_EPS, None, ALU.add).then_inc(x0_stat, 1)

            def x0_normalise(g):
                dve.wait_ge(x0_rstd, g + 1)
                for j in range(GP):
                    i = V.tensor_scalar(xn0[:, j, :], pair_of(X, g * GP + j), mv0[:, j, 0:1], rs0[:, j:j + 1],
                                        ALU.subtract, ALU.mult)
                i.then_inc(x0_norm, 1)

            def take_c(g1):
                dve.wait_ge(c_projected, g1)
                V.tensor_scalar(cq[:, :], RB[:, 0:GP], prod[:, 2:3], None, ALU.add).then_inc(cq_made, 1)

            dve.wait_ge(x_in, 32)
            x0_stats(0)
            x0_normalise(0)

            def mask_chunk(g, q, ahead, c):
                p, slot = g * GP + q + ahead, (q + ahead) % 2
                if c == 0:
                    dve.wait_ge(*pair_in(mb_here, g, q, 32, ahead))
                    if ahead:
                        dve.wait_ge(p_turned, p * SC)
                stand(scored, p * SC + c + 1)
                V.tensor_tensor_reduce(out=S[:, c * SN:(c + 1) * SN], in0=SB_[c][:, 0:SN],
                                       in1=mb[:, slot, c * SN:(c + 1) * SN], scale=1.0, scalar=-3.0e38,
                                       op0=ALU.add, op1=ALU.max, accum_out=pmax[:, c:c + 1]).then_inc(masked, 1)

            def shift(g, q, ahead):
                p, qn = g * GP + q + ahead, (q + ahead) % GP
                dve.wait_ge(masked, (p + 1) * SC)
                own(V.tensor_reduce(mfull[:, :], pmax[:, :], AX.X, ALU.max))
                if qn == 0:
                    dve.wait_ge(cq_made, g + 1 + ahead)
                own(V.tensor_scalar(mc[:, :], mfull[:, :], cq[:, qn:qn + 1], None, ALU.add))
                V.tensor_scalar(nbias[:, :], cq[:, qn:qn + 1], mc[:, 0:1], SCALE, ALU.subtract, ALU.mult)\
                    .then_inc(shifted, 1)

            def sum_rows(g, q):
                dve.wait_ge(exped, (g * GP + q + 1) * SC)
                V.tensor_reduce(rtot[:, :], rsum[:, :], AX.X, ALU.add).then_inc(rsum_read, 1)
                dve.wait_ge(rsum_read, g * GP + q + 1)
                own(V.reciprocal(rinv[:, :], rtot[:, :]))

            def make_o1(g, q):
                dve.wait_ge(pv_done, g * GP + q + 1)
                V.tensor_scalar(o1[:, :], OB, rinv[:, 0:1], None, ALU.mult).then_inc(o1_made, 1)

            def tail1(g, q):
                p1 = g * GP + q
                dve.wait_ge(projected, p1)
                V.tensor_tensor(a1, AB, bvo_bc[:, :], ALU.add).then_inc(a1_made, 1)
                dve.wait_ge(a1_made, p1)
                own(V.bn_stats(st1[:, :], a1), wait=stand)
                own(V.bn_aggr(mv1[:, :], st1[:, :]))
                V.tensor_scalar(ve1[:, :], mv1[:, 1:2], LN_EPS, None, ALU.add).then_inc(a_stat, 1)
                own(V.scalar_tensor_tensor(out=a2, in0=a1, scalar=mv1[:, 0:1], in1=g0_bc, op0=ALU.subtract, op1=ALU.mult))

            def tail2(g, q):
                p1 = g * GP + q
                dve.wait_ge(a_rstd, p1)
                dve.wait_ge(xb_made, p1)
                V.scalar_tensor_tensor(out=pair_of(X, p1 - 1), in0=a2, scalar=rs1[:, 0:1], in1=pair_of(X, p1 - 1),
                                       op0=ALU.mult, op1=ALU.add).then_inc(x1_made, 1)
                stand(x1_made, p1)
                own(V.bn_stats(st2[:, :], pair_of(X, p1 - 1)), wait=stand)
                own(V.bn_aggr(mv2[:, :], st2[:, :]))
                V.tensor_scalar(ve2[:, :], mv2[:, 1:2], 1.0 + RMS_EPS, LN_EPS * RMS_EPS, ALU.mult, ALU.add)\
                    .then_inc(x1_stat, 1)

            def tail3(g, q):
                p1 = g * GP + q
                dve.wait_ge(x1_rstd, p1)
                V.tensor_scalar(xn[:, (q - 1) % GP, :], pair_of(X, p1 - 1), mv2[:, 0:1], rs2[:, 0:1],
                                ALU.subtract, ALU.mult).then_inc(xn_made, 1)

            def split_x(g):
                dve.wait_ge(x_hi, g)
                V.tensor_tensor(xl[:, :], xT[:, :], xh[:, :].bitcast(F32), ALU.subtract).then_inc(x_split, 1)

            def combine1(g):
                dve.wait_ge(el_made, g)
                own(V.tensor_scalar(el[:, :, :], el[:, :, :], 1.0, None, ALU.add))
                own(V.reciprocal(pr[:, :, :], el[:, :, :]))
                for j in range(GP):
                    pj = pr[:, j, :].rearrange("p (o e) -> p o e", o=1).broadcast_to([PT2, NE, NE])
                    pe_ = pr[:, j, :].rearrange("p (e o) -> p e o", o=1).broadcast_to([PT2, NE, NE])
                    V.tensor_tensor(cmpg[:, j, :, :], pj, pe_, ALU.is_gt)
                    i = V.tensor_tensor(cmpe[:, j, :, :], pj, pe_, ALU.is_equal)
                own(i)

            def combine2(g):
                dve.wait_ge(pool_init, 3)
                lower = low[:, :, :].rearrange("p (o e) j -> p o e j", o=1).broadcast_to([PT2, GP, NE, NE])
                own(V.tensor_tensor(cmpe, cmpe, lower, ALU.mult))
                own(V.tensor_tensor(cmpg, cmpg, cmpe, ALU.add))
                own(V.tensor_reduce(rank, cmpg, AX.X, ALU.add))

            def combine3(g):
                own(V.scalar_tensor_tensor(out=selp[:, :, :], in0=rank, scalar=1.5, in1=pr[:, :, :],
                                           op0=ALU.is_lt, op1=ALU.mult))
                own(V.tensor_reduce(ssum[:, :], selp[:, :, :], AX.X, ALU.add))
                own(V.tensor_scalar(sden[:, :], ssum[:, :], 1e-6, None, ALU.add))
                own(V.reciprocal(sinv[:, :], sden[:, :]))
                for j in range(GP):
                    i = V.tensor_scalar(comb[:, :, j], selp[:, j, :], sinv[:, j:j + 1], None, ALU.mult)
                i.then_inc(comb_made, 1)

            def take_comb(g):
                dve.wait_ge(comb_turned, g)
                V.tensor_copy(combJ[:, :], MB[0:GP * NE, 0:PT2]).then_inc(combJ_made, 1)

            def split_h(g, n):
                f, r = g - 1, n % HR
                if n < UNITS and (hi_by_dve(n) or not lo_by_pool(n)):
                    dve.wait_ge(relued, f * UNITS + n + 1)
                    if hi_by_dve(n):
                        V.tensor_copy(Hh[:, r, :], Hf[:, n % 2, :]).then_inc(h_hi, 1)
                    if not lo_by_pool(n):
                        if hi_by_dve(n):
                            dve.wait_ge(*hi_made(f, n))
                        V.tensor_tensor(Hl[:, r, :], Hf[:, n % 2, :], Hh[:, r, :].bitcast(F32), ALU.subtract)\
                            .then_inc(h_split, 1)
                e = weighed_at(n)
                if e:
                    if e == 1:
                        dve.wait_ge(comb_here, 16 * g)
                    if e == 3:
                        dve.wait_ge(comb_rest_here, 16 * g)
                    if 3 <= e < NE:
                        dve.wait_ge(acc_added, f * (NE - 1) + e - 2)
                    dve.wait_ge(downed, f * UNITS + (e + 1) * MC)
                    w = comb_bc[:, (e - 1) * GT:e * GT]
                    if e < NE:
                        V.tensor_tensor(tmp[:, e % 2, :], YB[e % 2][:, 0:GT], w, ALU.mult).then_inc(y_read, 1)
                    else:
                        V.tensor_tensor(y_last[:, :, 0:SQ], YB[e % 2][:, 0:GT].rearrange("p (c i) -> p c i", i=SQ),
                                        w.rearrange("p (c i) -> p c i", i=SQ), ALU.mult).then_inc(y_read, 1)

            def finish(g):
                dve.wait_ge(y_turned, g)
                xg = X[:, bass.ds((g - 1) * GP, GP), :].rearrange("p j d -> p (j d)")
                V.tensor_tensor(xg, MB[:, :], xg, ALU.add).then_inc(out_made, 1)

            take_c(1)
            for c in range(SC):
                mask_chunk(0, 0, 0, c)
            shift(0, 0, 0)
            dve.wait_ge(setup_ev, 4)
            dve.wait_ge(rows_in, 16)
            V.tensor_tensor(bvo_bc[:, :], bv_wo, bo_bc, ALU.add).then_inc(dve_init, 1)
            dve.wait_ge(dve_init, 4)

            def body(kind, g):
                attn, ffn = has(kind, "attn"), has(kind, "ffn")
                for q in range(GP):
                    sa, sb1, sb2_ = steps_of(q) if ffn else ([], [], [])
                    scores_here = attn and (q < GP - 1 or has(kind, "next_q"))
                    tail = has_before(kind, q)
                    if attn:
                        sum_rows(g, q)
                    if tail:
                        tail1(g, q)
                    if kind == "first" and q == 2:
                        x0_normalise(g + 1)
                    for i, n in enumerate(sa):
                        split_h(g, n)
                        if tail and i == 0:
                            tail2(g, q)
                        if tail and i == 1:
                            tail3(g, q)
                        if i == 1 and q == GP - 1 and has(kind, "next_q"):
                            take_c(g + 2)
                    if not sa and q == GP - 1 and has(kind, "next_q"):
                        take_c(g + 2)
                    if scores_here:
                        for c in range(SC):
                            mask_chunk(g, q, 1, c)
                    if q == 0 and ffn:
                        split_x(g)
                    if scores_here:
                        shift(g, q, 1)
                    if q == 0 and ffn:
                        combine1(g)
                    if attn:
                        make_o1(g, q)
                    if kind == "first" and q == 1:
                        dve.wait_ge(x1_in, 32)
                        x0_stats(g + 1)
                    if tail and not ffn:
                        tail2(g, q)
                        tail3(g, q)
                    for i, n in enumerate(sb1 + sb2_):
                        split_h(g, n)
                        if q == 0 and i < 2:
                            (combine2, combine3)[i](g)
                        if q == 1 and i == 3 and has(kind, "next_q"):
                            dve.wait_ge(x_rest_in, 32)
                            x0_stats(g + 1)
                        if q == 2 and i == 1 and has(kind, "next_q"):
                            x0_normalise(g + 1)
                    if q == 0 and ffn:
                        take_comb(g)
                if attn:
                    tail1(g, GP)
                    tail2(g, GP)
                if kind == "late":
                    tail3(g, GP)
                if ffn:
                    finish(g)
                if attn and kind != "late":
                    tail3(g, GP)

            body("first", 0)
            straight = made[0]
            with dve.Fori(1, GROUPS - 1) as g:
                before[0] = (g - 1) * OWN_MID
                body("mid", g)
            assert made[0] - straight == OWN_MID, made[0] - straight
            before[0] = (GROUPS - 3) * OWN_MID
            body("late", GROUPS - 1)
            body("last", GROUPS)


OWN_MID = 44

_INS = ['x', 'ctx_1024', 'ctxT', 'mask_Bx1xS2_ik1', 'mats', 'cols', 'rows', 'L0_ffn_sw1', 'L0_ffn_sw2',
        'L0_ffn_sb2', 'L0_ffn_ew1', 'L0_ffn_ew2', 'L0_ffn_eb2']


def kernel(**inputs):
    import numpy as np
    import concourse.bacc as bacc
    from concourse.bass_utils import run_bass_kernel_spmd

    a = {k: np.asarray(v) for k, v in inputs.items()}
    a['ctxT'] = a['ctx_1024'].transpose(0, 2, 1)
    a['mats'] = np.concatenate([a['L0_xattn_Wq'].T, a['L0_xattn_Wk'].T, a['L0_xattn_Wv'].T, a['L0_xattn_Wo'],
                                np.eye(P, dtype=np.float32)], axis=1)
    a['cols'] = np.concatenate([a['L0_xattn_bq'][:, None], a['L0_xattn_bk'][:, None], a['L0_xattn_bv'][:, None],
                                a['L0_ffn_norm_weight'][:, None], a['L0_ffn_router_w'].T,
                                a['L0_ffn_sb1'].reshape(MC, P).T, a['L0_ffn_eb1'].reshape(NE * MC, P).T], axis=1)
    a['rows'] = np.concatenate([a['L0_xattn_bo'], a['L0_xattn_g0'], a['L0_xattn_beta0']])
    nc = bacc.Bacc("TRN2", target_bir_lowering=False, num_devices=1)
    arrays, args = {}, []
    for name in _INS:
        v = np.ascontiguousarray(a[name])
        arrays[f"in_{name}_dram"] = v
        args.append(nc.dram_tensor(f"in_{name}_dram", v.shape, mybir.dt.from_np(v.dtype), kind="ExternalInput").ap())
    out = nc.dram_tensor("out_dram", (B, SQ, D), F32, kind="ExternalOutput").ap()
    build(nc, *args, out)
    r = run_bass_kernel_spmd(nc, [arrays], core_ids=[0])
    return r.results[0]["out_dram"]
```
